# Optimizing a Trainium2 kernel written in Bass

```python
import numpy as np
import jax
import jax.numpy as jnp

def _softmax(x, axis=-1):
    return jax.nn.softmax(x, axis=axis)
def _gelu(x):
    return jax.nn.gelu(x, approximate=True)
def _silu(x):
    return jax.nn.silu(x)
def _sigmoid(x):
    return jax.nn.sigmoid(x)
def _layernorm(x, axis=-1, eps=1e-5):
    m = jnp.mean(x, axis=axis, keepdims=True)
    v = jnp.var(x, axis=axis, keepdims=True)
    return (x - m) / jnp.sqrt(v + eps)
def _scatter_add(tgt, idx, src, axis=0):
    return tgt.at[idx].add(src)
def _segment_sum(src, seg, n):
    return jax.ops.segment_sum(src, seg, n)

kernel_name = 'mk_conv_seq_d1_conv_nchw512_3166ad'

def setup_inputs(seed: int = 0):
    np.random.seed(seed)
    _w = jnp.asarray
    def _rec_inputs():
        import jax
        import jax.numpy as jnp
        _gk = jax.random.key(seed)
        x = 7.22e-05 + 1 * jax.random.normal(jax.random.fold_in(_gk, 1), (16, 512, 32, 32), jnp.float32)
        return x
    x = _rec_inputs()
    def _L0_conv_setup():
        import jax, jax.numpy as jnp
        import numpy as np
        import math
        C = 512
        G = 32
        EPS = 1e-05

        def _group_norm(x, gamma, beta):
            b, c, h, w = x.shape
            xg = x.reshape(b, G, c // G * h * w)
            mu = jnp.mean(xg, axis=-1, keepdims=True)
            var = jnp.var(xg, axis=-1, keepdims=True)
            xn = ((xg - mu) / jnp.sqrt(var + EPS)).reshape(b, c, h, w)
            return xn * gamma[None, :, None, None] + beta[None, :, None, None]
        key = jax.random.key(seed)
        ks = jax.random.split(key, 7)
        B, H, W = (16, 32, 32)
        x = jax.random.normal(ks[0], (B, C, H, W), dtype=jnp.float32)
        gamma = jnp.ones((C,), dtype=jnp.float32)
        beta = jnp.zeros((C,), dtype=jnp.float32)
        fan = 1.0 / math.sqrt(C)
        qkv_w = jax.random.uniform(ks[1], (3 * C, C), minval=-fan, maxval=fan, dtype=jnp.float32)
        qkv_b = jax.random.uniform(ks[2], (3 * C,), minval=-fan, maxval=fan, dtype=jnp.float32)
        proj_w = jax.random.uniform(ks[3], (C, C), minval=-fan, maxval=fan, dtype=jnp.float32)
        proj_b = jax.random.uniform(ks[4], (C,), minval=-fan, maxval=fan, dtype=jnp.float32)
        return {'x': x, 'gamma': gamma, 'beta': beta, 'qkv_w': qkv_w, 'qkv_b': qkv_b, 'proj_w': proj_w, 'proj_b': proj_b}
    _L0_conv_all = _L0_conv_setup()
    _L0_conv_in = {k: v for k, v in _L0_conv_all.items() if k in ('gamma', 'beta', 'qkv_w', 'qkv_b', 'proj_w', 'proj_b', )}
    del _L0_conv_all

    return {
        "x": x,
        "L0_conv_gamma": _L0_conv_in["gamma"],
        "L0_conv_beta": _L0_conv_in["beta"],
        "L0_conv_qkv_w": _L0_conv_in["qkv_w"],
        "L0_conv_qkv_b": _L0_conv_in["qkv_b"],
        "L0_conv_proj_w": _L0_conv_in["proj_w"],
        "L0_conv_proj_b": _L0_conv_in["proj_b"],
    }

def reference(x, L0_conv_gamma, L0_conv_beta, L0_conv_qkv_w, L0_conv_qkv_b, L0_conv_proj_w, L0_conv_proj_b):
    import jax
    import jax.numpy as jnp
    def _L0_conv_ref(x, gamma, beta, qkv_w, qkv_b, proj_w, proj_b):
        import jax, jax.numpy as jnp
        import numpy as np
        import math
        C = 512
        G = 32
        EPS = 1e-05

        def _group_norm(x, gamma, beta):
            b, c, h, w = x.shape
            xg = x.reshape(b, G, c // G * h * w)
            mu = jnp.mean(xg, axis=-1, keepdims=True)
            var = jnp.var(xg, axis=-1, keepdims=True)
            xn = ((xg - mu) / jnp.sqrt(var + EPS)).reshape(b, c, h, w)
            return xn * gamma[None, :, None, None] + beta[None, :, None, None]
        b, c, h, w = x.shape
        hn = _group_norm(x, gamma, beta)
        qkv = jnp.einsum('bchw,oc->bohw', hn, qkv_w) + qkv_b[None, :, None, None]
        q, k, v = jnp.split(qkv, 3, axis=1)
        q = q.reshape(b, c, h * w).transpose(0, 2, 1)
        k = k.reshape(b, c, h * w).transpose(0, 2, 1)
        v = v.reshape(b, c, h * w).transpose(0, 2, 1)
        scale = 1.0 / math.sqrt(c)
        attn = jax.nn.softmax(jnp.einsum('bnc,bmc->bnm', q, k) * scale, axis=-1)
        out = jnp.einsum('bnm,bmc->bnc', attn, v)
        out = out.transpose(0, 2, 1).reshape(b, c, h, w)
        out = jnp.einsum('bchw,oc->bohw', out, proj_w) + proj_b[None, :, None, None]
        return x + out

    def _gn(v, G=32, eps=1e-5):
        B_, C_, H_, W_ = v.shape
        g = v.reshape(B_, G, C_ // G, H_, W_)
        m = jnp.mean(g, axis=(2, 3, 4), keepdims=True)
        s = jnp.var(g, axis=(2, 3, 4), keepdims=True)
        return ((g - m) / jnp.sqrt(s + eps)).reshape(v.shape)

    def _ln_c(v, eps=1e-6):
        m = jnp.mean(v, axis=1, keepdims=True)
        s = jnp.var(v, axis=1, keepdims=True)
        return (v - m) / jnp.sqrt(s + eps)

    def _ln_t(v, eps=1e-5):
        m = jnp.mean(v, axis=-1, keepdims=True)
        s = jnp.var(v, axis=-1, keepdims=True)
        return (v - m) / jnp.sqrt(s + eps)

    def _to_tokens(v):
        B_, C_, H_, W_ = v.shape
        return v.reshape(B_, C_, H_ * W_).transpose(0, 2, 1)
    def _from_tokens(t, like):
        B_, C_, H_, W_ = like.shape
        return t.transpose(0, 2, 1).reshape(B_, C_, H_, W_)

    x = _L0_conv_ref(x, L0_conv_gamma, L0_conv_beta, L0_conv_qkv_w, L0_conv_qkv_b, L0_conv_proj_w, L0_conv_proj_b)
    return x


_drawn_inputs = setup_inputs


def setup_inputs(seed=0):
    import zlib

    import numpy as np

    out = dict(_drawn_inputs(seed))
    spreads = {'L0_conv_gamma': (1.0, 0.6), 'L0_conv_beta': (0.0, 0.1)}
    factors = {'L0_conv_qkv_b': 3.791}
    for name, (base, spread) in spreads.items():
        noise = np.random.default_rng([zlib.crc32(name.encode()), seed]).standard_normal(out[name].shape)
        drawn = base * np.exp(spread * noise) if base else spread * noise
        out[name] = jnp.asarray(drawn.astype(out[name].dtype))
    for name, factor in factors.items():
        out[name] = (out[name] * factor).astype(out[name].dtype)
    return out
```

```python
import math
from contextlib import ExitStack

import concourse.bass as bass
from concourse import mybir


def attention_block_kernel(nc, x, gamma, beta, qkv_w, qkv_b, proj_w, proj_b, out):
    fp32, fp16, i32 = mybir.dt.float32, mybir.dt.float16, mybir.dt.int32
    ALU, ACT, AX = mybir.AluOpType, mybir.ActivationFunctionType, mybir.AxisListType

    P = 128
    NB, C, HH, WW = x.shape
    N = HH * WW
    GROUP = C // 32
    EPS = 1e-5
    CT, MT = C // P, N // P
    H = 512
    NH = N // H
    KC = 2
    NK = MT // KC
    Q = 32
    SCALE = 1.0 / math.sqrt(C)
    XMAX = 128.0
    W_TOP = 2.0 ** 14
    T_TOP = 2.0 ** 15
    NEWTON = 4
    STATS = 9 + 3 * NEWTON
    U_SCALE = T_TOP / (C * XMAX * W_TOP)
    P_LOG = 12 * math.log(2.0)

    MB = 5
    BATCH = ([("s", i) for i in range(NH * MT)] + [("t", i) for i in range(CT * NH)]
             + [("o", i) for i in range(NH * CT)] + [("u", i) for i in range(MT)])
    LAST = [g for g in BATCH if g[0] in "so"]
    PROLOGUE = [g for g in BATCH if g[0] in "tu"]
    PER = {"s": NH * MT, "t": CT * NH, "o": NH * CT, "u": MT}
    assert len(BATCH) % MB == 0
    BASE = len(PROLOGUE) % MB

    x_d = x.rearrange("b (t p) h w -> b p t (h w)", p=P)
    out_d = out.rearrange("b (t p) h w -> b p t (h w)", p=P)

    ctx = ExitStack()
    with ctx:
        def sb(name, shape, dt=fp32):
            return ctx.enter_context(nc.sbuf_tensor(name, shape, dt))

        def pb(name):
            return ctx.enter_context(nc.psum_tensor(name, [P, 512], fp32))

        def sem(name):
            return ctx.enter_context(nc.semaphore(name))

        xs = [sb(f"x{p}", [P, CT, N]) for p in range(2)]
        xh = [sb(f"xh{p}", [P, CT, N], fp16) for p in range(2)]
        xl = [sb(f"xl{p}", [P, CT, N], fp16) for p in range(2)]
        xf = sb("xf", [P, 2, N])
        th = sb("th", [P, CT, N], fp16)
        tl = sb("tl", [P, CT, N], fp16)
        tf = sb("tf", [P, 4, H])
        uh = sb("uh", [P, MT, C], fp16)
        ul = sb("ul", [P, MT, C], fp16)
        sp = [sb(f"sp{h}", [P, MT, H]) for h in range(NH)]
        pf = sb("pf", [P, 2, KC, H])
        ah = sb("ah", [P, CT, C], fp16)
        al = sb("al", [P, CT, C], fp16)
        bh = sb("bh", [P, CT, C], fp16)
        bl = sb("bl", [P, CT, C], fp16)
        ob = sb("ob", [P, CT, H])
        mx = sb("mx", [P, 2, H])
        tr = sb("tr", [P, H])
        maxb = sb("maxb", [P, H])
        ps2 = sb("ps2", [P, KC, H])
        sf = sb("sf", [P, H])
        sh = sb("sh", [P, H], fp16)
        sl = sb("sl", [P, H], fp16)
        rinv = sb("rinv", [P, H])
        gacc = sb("gacc", [P, N])
        gcol = sb("gcol", [P, MT])
        st = sb("st", [P, CT, 2, 6])
        mv = sb("mv", [P, CT, 2])
        dev = sb("dev", [P, CT])
        var = sb("var", [P, CT])
        rs = sb("rs", [P, CT])
        nt = sb("nt", [P, CT])
        mg = sb("mg", [P, CT])
        nb = sb("nb", [P, CT])
        rq = sb("rq", [P, H // Q])
        rg = sb("rg", [Q, P // Q, H // Q])
        r1 = sb("r1", [Q, H // Q])
        mb = sb("mb", [P, H // Q])
        ident = sb("ident", [P, P])
        gmean = sb("gmean", [P, P])
        ones = sb("ones", [P, P])
        ones16 = sb("ones16", [P, P], fp16)
        ebias = sb("ebias", [P, 1])
        gam = sb("gam", [P, CT])
        qkvb = sb("qkvb", [P, 3 * CT])
        projb = sb("projb", [P, CT])
        bdot = sb("bdot", [P, 3 * CT])
        bt = sb("bt", [P, 3 * CT])
        prod = sb("prod", [P, CT])
        am = sb("am", [P, 3])
        amr = sb("amr", [P, 3])
        s0 = sb("s0", [P, 4])
        s1 = sb("s1", [P, 4])
        sc = sb("sc", [P, 4])
        si = sb("si", [P, 4])
        ft = sb("ft", [P, 1])
        esc = sb("esc", [P, 1])
        cu = sb("cu", [P, 1])
        tv = sb("tv", [P, 4 * CT])
        ta = sb("ta", [P, CT])
        gw = sb("gw", [P, CT])
        gc = sb("gc", [P, 1])
        obias = sb("obias", [P, CT])
        w_qkv = [sp[0][:, 0:CT, :], sp[0][:, CT:2 * CT, :], sp[1][:, 0:CT, :]]
        w_p = sp[1][:, CT:2 * CT, :]
        w_pt = pf[:, :, :, :].rearrange("p a b n -> p (a b) n")
        at32 = xs[1][:, 0:2, :].rearrange("p a (b n) -> p (a b) n", n=C)
        bt32 = xs[1][:, 2:4, :].rearrange("p a (b n) -> p (a b) n", n=C)
        gam_row, beta_row, junk = tf[:, 0, :], tf[:, 1, :], tf[:, 2, :]

        bank = [pb(f"bank{i}") for i in range(MB)]
        ps_sum, ps_g, ps_small = pb("ps_sum"), pb("ps_g"), pb("ps_small")

        small_in, wqk_in, wp_in, wv_in = sem("small_in"), sem("wqk_in"), sem("wp_in"), sem("wv_in")
        x_in = [sem("x_in0"), sem("x_in1")]
        masks, consts, row_in = sem("masks"), sem("consts"), sem("row_in")
        set_full, set_evac, set_step = sem("set_full"), sem("set_evac"), sem("set_step")
        vec_full, absmax, scratch_free = sem("vec_full"), sem("absmax"), sem("scratch_free")
        am_ready, bias_qk, bias_v = sem("am_ready"), sem("bias_qk"), sem("bias_v")
        full = {k: sem(f"{k}_full") for k in "stou"}
        evac = {k: sem(f"{k}_evac") for k in "stou"}
        stat_step, stat_pe = sem("stat_step"), sem("stat_pe")
        rs_ready, xf_done, xh_done, xl_done = sem("rs_ready"), sem("xf_done"), sem("xh_done"), sem("xl_done")
        xf_free, g_step, g_full, g_ready = sem("xf_free"), sem("g_step"), sem("g_full"), sem("g_ready")
        tf_done, tl_done, uh_done = sem("tf_done"), sem("tl_done"), sem("uh_done")
        split_ready = sem("split_ready")
        max_step, max_ready, mat_a, sub_done, pf_done, ph_done = sem("max_step"), sem("max_ready"), sem("mat_a"), sem("sub_done"), sem("pf_done"), sem("ph_done")
        pl_done, sum_step, sum_split, sum_full, rinv_done = (
            sem("pl_done"), sem("sum_step"), sem("sum_split"), sem("sum_full"), sem("rinv_done"))
        out_ready, stored = sem("out_ready"), sem("stored")

        def count(per, batch, off):
            reg, c = batch
            return per * c + off if reg is None else reg * per + (per * c + off)

        def wait(eng, s, per, batch, off):
            reg, c = batch
            if reg is None:
                if per * c + off > 0:
                    eng.wait_ge(s, per * c + off)
            else:
                assert per * (c + 1) + off > 0
                eng.wait_ge(s, count(per, batch, off))

        def parity(batch):
            reg, c = batch
            return c % 2 if reg is None else (c + 1) % 2

        def nxt(batch):
            return batch[0], batch[1] + 1

        def chunk(h, k):
            v = sp[h][:, KC * k:KC * k + KC, :].bitcast(fp16).rearrange("p a n -> p (a n)")
            return v[:, 0:KC * H], v[:, KC * H:2 * KC * H]

        def batches(eng, one):
            one((None, 0), False)
            with eng.Fori(1, NB - 2, 2) as r:
                one((r, 0), False)
                one((r, 1), False)
            one((None, NB - 1), True)

        block = ctx.enter_context(nc.Block())

        @block.sync
        def _(sp_eng):
            wv = qkv_w.rearrange("(s t p) c -> s p t c", s=3, p=P)
            sp_eng.dma_start(w_qkv[0], wv[0]).then_inc(wqk_in, 16)
            sp_eng.dma_start(w_qkv[1], wv[1]).then_inc(wqk_in, 16)
            sp_eng.dma_start(w_p, proj_w.rearrange("(t p) c -> p t c", p=P)).then_inc(wp_in, 16)
            sp_eng.dma_start(w_qkv[2], wv[2]).then_inc(wv_in, 16)
            sp_eng.dma_start(xs[0][:, :, :], x_d[0]).then_inc(x_in[0], 16)

            def one(b, last):
                if not last:
                    nxt_b = nxt(b)
                    if b[0] is None and b[1] == 0:
                        sp_eng.wait_ge(scratch_free, 1)
                    wait(sp_eng, out_ready, PER["o"], b, 0)
                    src = x_d[1] if b[0] is None else x_d[b[0] + nxt_b[1]]
                    sp_eng.dma_start(xs[parity(nxt_b)][:, :, :], src).then_inc(x_in[parity(nxt_b)], 16)
                for h in range(NH):
                    wait(sp_eng, out_ready, PER["o"], b, CT * (h + 1))
                    dst = out_d[b[1]] if b[0] is None else out_d[b[0] + b[1]]
                    sp_eng.dma_start(dst[:, :, h * H:(h + 1) * H], ob[:, :, :]).then_inc(stored, 16)

            batches(sp_eng, one)
            sp_eng.wait_ge(stored, 16 * NH * NB)

        @block.gpsimd
        def _(pool):
            nc.gpsimd.memset(ident[:, :], 0.0).then_inc(masks, 1)
            nc.gpsimd.memset(gmean[:, :], 1.0 / GROUP).then_inc(masks, 1)
            nc.gpsimd.memset(ones[:, :], 1.0).then_inc(consts, 1)
            nc.gpsimd.memset(ones16[:, :], 1.0).then_inc(consts, 1)
            nc.gpsimd.memset(ebias[:, :], P_LOG).then_inc(consts, 1)
            pool.wait_ge(masks, 2)
            nc.gpsimd.affine_select(out=ident[:, :], in_=ident[:, :], compare_op=ALU.not_equal, fill=1.0,
                                    base=0, pattern=[[-1, P]], channel_multiplier=1).then_inc(consts, 1)
            blocks = gmean[:, :].rearrange("p (g j) -> p g j", j=GROUP)
            nc.gpsimd.affine_select(out=blocks, in_=blocks, compare_op=ALU.is_ge, fill=0.0, base=0,
                                    pattern=[[-GROUP, P // GROUP], [0, GROUP]], channel_multiplier=1).then_inc(masks, 1)
            pool.wait_ge(masks, 3)
            nc.gpsimd.affine_select(out=blocks, in_=blocks, compare_op=ALU.is_ge, fill=0.0, base=GROUP - 1,
                                    pattern=[[GROUP, P // GROUP], [0, GROUP]], channel_multiplier=-1).then_inc(consts, 1)
            pool.wait_ge(am_ready, 1)
            nc.gpsimd.partition_all_reduce(amr[:, :], am[:, :], P, bass.bass_isa.ReduceOp.absmax).then_inc(absmax, 1)

        @block.scalar
        def _(act):
            with nc.allow_non_contiguous_dma(reason="biases, a value per partition"):
                act.dma_start(gam[:, :], gamma.rearrange("(t p) -> p t", p=P)).then_inc(small_in, 16)
                act.dma_start(qkvb[:, :], qkv_b.rearrange("(t p) -> p t", p=P)).then_inc(small_in, 16)
                act.dma_start(projb[:, :], proj_b.rearrange("(t p) -> p t", p=P)).then_inc(small_in, 16)
            act.dma_start(gam_row, gamma.partition_broadcast(P)).then_inc(row_in, 16)
            act.dma_start(beta_row, beta.partition_broadcast(P)).then_inc(row_in, 16)

            def x_norm(bn, c):
                p = parity(bn)
                wait(act, rs_ready, 1, bn, 1)
                wait(act, xf_free, CT, bn, c - 1)
                nc.scalar.activation(xf[:, c % 2, :], xs[p][:, c, :], ACT.Identity,
                                     bias=nb[:, c:c + 1], scale=rs[:, c:c + 1]).then_inc(xf_done, 1)
                nc.scalar.activation(xh[p][:, c, :], xs[p][:, c, :], ACT.Identity,
                                     bias=nb[:, c:c + 1], scale=rs[:, c:c + 1]).then_inc(xh_done, 1)

            def t_group(bn, i, bk):
                ct, mh = i // NH, i % NH
                wait(act, full["t"], PER["t"], bn, i + 1)
                wait(act, tl_done, PER["t"], bn, i - 3)
                nc.scalar.activation(tf[:, i % 4, :], bk[:, :], ACT.Identity,
                                     bias=ta[:, ct:ct + 1], scale=ft[:, 0:1]).then_inc(tf_done, 1)
                nc.scalar.activation(th[:, ct, mh * H:(mh + 1) * H], bk[:, :], ACT.Identity,
                                     bias=ta[:, ct:ct + 1], scale=ft[:, 0:1]).then_inc(evac["t"], 1)

            def u_group(bn, i, bk):
                wait(act, full["u"], PER["u"], bn, i + 1)
                nc.scalar.activation(uh[:, i, :], bk[:, :], ACT.Copy, scale=U_SCALE).then_inc(uh_done, 1)

            def s_group(b, i, bk):
                h, mt = i // MT, i % MT
                wait(act, full["s"], PER["s"], b, i + 1)
                if i == 0:
                    wait(act, g_ready, 1, b, 1)
                if mt == 0:
                    wait(act, full["o"], PER["o"], b, CT * (h + 1) - PER["o"])
                nc.scalar.activation(sp[h][:, mt, :], bk[:, :], ACT.Identity,
                                     bias=gcol[:, mt:mt + 1]).then_inc(evac["s"], 1)

            def exps(b, h, k):
                n = NK * h + k
                wait(act, sub_done, NH * NK, b, n + 1)
                wait(act, sum_step, NH * (NK + 1), b, (NK + 1) * h + (max(k - 2, 1) if k >= 2 else k + NK - 2 - (NK + 1)))
                nc.scalar.activation(pf[:, k % 2, :, :], sp[h][:, KC * k:KC * k + KC, :], ACT.Exp,
                                     bias=ebias[:, 0:1], scale=esc[:, 0:1]).then_inc(pf_done, 1)

            def high(b, h, k):
                wait(act, pf_done, NH * NK, b, NK * h + k + 1)
                hi, _ = chunk(h, k)
                nc.scalar.activation(hi, pf[:, k % 2, :, :].rearrange("p a n -> p (a n)"), ACT.Copy).then_inc(ph_done, 1)

            b0 = (None, 0)
            act.wait_ge(consts, 5)
            act.wait_ge(split_ready, 1)
            for c in range(CT):
                x_norm(b0, c)
            for g, (kind, i) in enumerate(PROLOGUE):
                (t_group if kind == "t" else u_group)(b0, i, bank[g % MB])

            def one(b, last):
                bn = nxt(b)
                seq = LAST if last else BATCH
                bk = {g: bank[(BASE + n) % MB] for n, g in enumerate(seq)}
                for i in range(MT):
                    s_group(b, i, bk["s", i])
                s1_order = ["S0", "S1", "E0", "S2", "E1", "S3", "X0", "S4", "X1", "S5", "X2", "S6", "X3", "S7"]
                for step in s1_order:
                    n = int(step[1])
                    if step[0] == "S":
                        s_group(b, MT + n, bk["s", MT + n])
                    elif step[0] == "E":
                        exps(b, 0, n)
                    elif not last:
                        x_norm(bn, n)
                t_order = ["H00", "H01", "T0", "E02", "T1", "E03", "H02", "T2", "H03", "T3", "T4",
                           "E10", "T5", "E11", "T6", "H10", "T7", "H11", "E12", "H12", "E13", "H13"]
                for step in t_order:
                    if step[0] == "T":
                        if not last:
                            t_group(bn, int(step[1]), bk["t", int(step[1])])
                    else:
                        (exps if step[0] == "E" else high)(b, int(step[1]), int(step[2]))
                if not last:
                    for i in range(MT):
                        u_group(bn, i, bk["u", i])

            batches(act, one)

        @block.vector
        def _(dve):
            v = nc.vector
            steps = [0]

            def link(ins):
                steps[0] += 1
                ins.then_inc(set_step, 1)
                dve.wait_ge(set_step, steps[0])

            def stats(bn, i):
                p = parity(bn)
                if i == 0:
                    wait(dve, x_in[p], 8, bn, 16 - 8 * p)
                ins = v.bn_stats(st[:, i // 2, i % 2, :], xs[p][:, i // 2, (i % 2) * 512:(i % 2 + 1) * 512])
                if i == 2 * CT - 1:
                    ins.then_inc(stat_step, 1)

            def norm_a(bn):
                for c in range(CT):
                    ins = v.bn_aggr(mv[:, c, :], st[:, c, :, :].rearrange("p a b -> p (a b)"))
                ins.then_inc(stat_step, 1)

            def norm_b(bn):
                wait(dve, stat_pe, 2, bn, 1)
                v.tensor_copy(mg[:, :], ps_small[:, 0:CT]).then_inc(stat_step, 1)
                wait(dve, stat_step, STATS, bn, 3)
                v.tensor_tensor(dev[:, :], mv[:, :, 0], mg[:, :], ALU.subtract).then_inc(stat_step, 1)
                wait(dve, stat_step, STATS, bn, 4)
                v.tensor_tensor(var[:, :], dev[:, :], dev[:, :], ALU.mult).then_inc(stat_step, 1)
                wait(dve, stat_step, STATS, bn, 5)
                v.tensor_tensor(dev[:, :], var[:, :], mv[:, :, 1], ALU.add).then_inc(stat_step, 1)

            def norm_c(bn):
                wait(dve, stat_pe, 2, bn, 2)
                v.tensor_scalar(var[:, :], ps_small[:, CT:2 * CT], EPS, None, ALU.add).then_inc(stat_step, 1)
                wait(dve, stat_step, STATS, bn, 7)
                v.tensor_single_scalar(nt[:, :].bitcast(i32), var[:, :].bitcast(i32), 1,
                                       ALU.logical_shift_right).then_inc(stat_step, 1)
                wait(dve, stat_step, STATS, bn, 8)
                v.tensor_scalar(rs[:, :].bitcast(i32), nt[:, :].bitcast(i32), -1.0, float(0x5F3759DF),
                                ALU.mult, ALU.add).then_inc(stat_step, 1)
                for k in range(NEWTON):
                    wait(dve, stat_step, STATS, bn, 9 + 3 * k)
                    v.tensor_tensor(nt[:, :], rs[:, :], rs[:, :], ALU.mult).then_inc(stat_step, 1)
                    wait(dve, stat_step, STATS, bn, 10 + 3 * k)
                    v.scalar_tensor_tensor(out=dev[:, :], in0=nt[:, :], scalar=-0.5, in1=var[:, :],
                                           op0=ALU.mult, op1=ALU.mult).then_inc(stat_step, 1)
                    wait(dve, stat_step, STATS, bn, 11 + 3 * k)
                    v.scalar_tensor_tensor(out=rs[:, :], in0=dev[:, :], scalar=1.5, in1=rs[:, :],
                                           op0=ALU.add, op1=ALU.mult).then_inc(stat_step, 1)
                wait(dve, stat_step, STATS, bn, STATS)
                v.scalar_tensor_tensor(out=nb[:, :], in0=mg[:, :], scalar=-1.0, in1=rs[:, :],
                                       op0=ALU.mult, op1=ALU.mult).then_inc(rs_ready, 1)

            def x_low(bn, c):
                p = parity(bn)
                wait(dve, xf_done, CT, bn, c + 1)
                wait(dve, xh_done, CT, bn, c + 1)
                v.tensor_tensor(xl[p][:, c, :], xf[:, c % 2, :], xh[p][:, c, :], ALU.subtract).then_inc(xl_done, 1)
                if c == 0:
                    wait(dve, g_full, 1, bn, 0)
                    v.tensor_scalar(gacc[:, :], xf[:, 0, :], gw[:, 0:1], None, ALU.mult).then_inc(xf_free, 1)
                else:
                    wait(dve, xf_free, CT, bn, c)
                    v.scalar_tensor_tensor(out=gacc[:, :], in0=xf[:, c % 2, :], scalar=gw[:, c:c + 1],
                                           in1=gacc[:, :], op0=ALU.mult, op1=ALU.add).then_inc(xf_free, 1)

            def g_columns(bn):
                wait(dve, g_full, 1, bn, 1)
                v.tensor_scalar(gcol[:, :], ps_g[:, 0:MT], gc[:, 0:1], None, ALU.add).then_inc(g_ready, 1)

            def t_low(bn, i):
                ct, mh = i // NH, i % NH
                wait(dve, tf_done, PER["t"], bn, i + 1)
                wait(dve, evac["t"], PER["t"], bn, i + 1)
                v.tensor_tensor(tl[:, ct, mh * H:(mh + 1) * H], tf[:, i % 4, :], th[:, ct, mh * H:(mh + 1) * H],
                                ALU.subtract).then_inc(tl_done, 1)

            def u_low(bn, i, bk):
                wait(dve, uh_done, PER["u"], bn, i + 1)
                v.scalar_tensor_tensor(out=ul[:, i, :], in0=bk[:, :], scalar=U_SCALE, in1=uh[:, i, :],
                                       op0=ALU.mult, op1=ALU.subtract).then_inc(evac["u"], 1)

            MAXES = 9

            def max_part(b, h, k):
                if k == 0:
                    return
                a, c = NH * MAXES, MAXES * h
                wait(dve, evac["s"], PER["s"], b, MT * h + KC * (k + 1))
                if k >= 2:
                    wait(dve, max_step, a, b, c + k - 1)
                first = sp[h][:, 0:KC, :] if k == 1 else mx[:, :, :]
                v.tensor_tensor(mx[:, :, :], first, sp[h][:, KC * k:KC * k + KC, :], ALU.max).then_inc(max_step, 1)

            def max_pair(b, h):
                wait(dve, max_step, NH * MAXES, b, MAXES * h + 3)
                v.tensor_tensor(mx[:, 0, :], mx[:, 0, :], mx[:, 1, :], ALU.max).then_inc(max_step, 1)

            def max_all(b, h):
                a, c = NH * MAXES, MAXES * h
                wait(dve, max_step, a, b, c + 4)
                v.transpose(tr[:, :], mx[:, 0, :]).then_inc(max_step, 1)
                wait(dve, max_step, a, b, c + 5)
                v.tensor_reduce(rq[:, :], tr[:, :].rearrange("p (k i) -> p k i", i=Q), axis=AX.X,
                                op=ALU.max).then_inc(max_step, 1)
                wait(dve, max_step, a, b, c + 6)
                for q in range(P // Q):
                    ins = v.tensor_copy(rg[:, q, :], rq[Q * q:Q * q + Q, :])
                ins.then_inc(max_step, 1)
                wait(dve, max_step, a, b, c + 7)
                v.tensor_reduce(r1[:, :], rg[:, :, :].rearrange("p q k -> p k q"), axis=AX.X,
                                op=ALU.max).then_inc(max_step, 1)
                wait(dve, max_step, a, b, c + 8)
                for q in range(P // Q):
                    ins = v.tensor_copy(mb[Q * q:Q * q + Q, :], r1[:, :])
                ins.then_inc(max_step, 1)
                wait(dve, max_step, a, b, c + 9)
                v.transpose(maxb[:, :].rearrange("p (k i) -> p k i", i=Q),
                            mb[:, :].unsqueeze(2).to_broadcast([P, H // Q, Q])).then_inc(max_ready, 1)

            def sub(b, h, k):
                if k == 0:
                    wait(dve, max_ready, NH, b, h + 1)
                tile = sp[h][:, KC * k:KC * k + KC, :]
                v.tensor_tensor(tile, tile, maxb[:, :].unsqueeze(1).to_broadcast([P, KC, H]),
                                ALU.subtract).then_inc(sub_done, 1)

            def split(b, h, k):
                a, c = NH * (NK + 1), (NK + 1) * h
                wait(dve, ph_done, NH * NK, b, NK * h + k + 1)
                hi, lo = chunk(h, k)
                v.tensor_tensor(lo, pf[:, k % 2, :, :].rearrange("p a n -> p (a n)"), hi, ALU.subtract).then_inc(pl_done, 1)
                if k == 1:
                    v.tensor_tensor(ps2[:, :, :], pf[:, 0, :, :], pf[:, 1, :, :], ALU.add).then_inc(sum_step, 1)
                elif k >= 2:
                    wait(dve, sum_step, a, b, c + k - 1)
                    v.tensor_tensor(ps2[:, :, :], ps2[:, :, :], pf[:, k % 2, :, :], ALU.add).then_inc(sum_step, 1)

            def sum_parts(b, h):
                a, c = NH * (NK + 1), (NK + 1) * h
                wait(dve, sum_step, a, b, c + 3)
                v.tensor_tensor(sf[:, :], ps2[:, 0, :], ps2[:, 1, :], ALU.add).then_inc(sum_step, 1)
                wait(dve, sum_step, a, b, c + 4)
                wait(dve, sum_full, NH, b, h)
                v.tensor_copy(sh[:, :], sf[:, :]).then_inc(sum_step, 1)
                wait(dve, sum_step, a, b, c + 5)
                v.tensor_tensor(sl[:, :], sf[:, :], sh[:, :], ALU.subtract).then_inc(sum_split, 1)

            def inverse(b, h):
                wait(dve, sum_full, NH, b, h + 1)
                v.reciprocal(rinv[:, :], ps_sum[:, :]).then_inc(rinv_done, 1)

            def out_group(b, i, bk):
                h, c = i // CT, i % CT
                wait(dve, full["o"], PER["o"], b, i + 1)
                if c == 0:
                    wait(dve, rinv_done, NH, b, h + 1)
                    wait(dve, stored, 16 * NH, b, 16 * h)
                v.scalar_tensor_tensor(out=ob[:, c, :], in0=bk[:, :], scalar=cu[:, 0:1], in1=rinv[:, :],
                                       op0=ALU.mult, op1=ALU.mult).then_inc(evac["o"], 1)
                wait(dve, evac["o"], PER["o"], b, i + 1)
                v.scalar_tensor_tensor(out=ob[:, c, :], in0=ob[:, c, :], scalar=obias[:, c:c + 1],
                                       in1=xs[parity(b)][:, c, h * H:(h + 1) * H],
                                       op0=ALU.add, op1=ALU.add).then_inc(out_ready, 1)

            b0 = (None, 0)
            dve.wait_ge(row_in, 32)
            dve.wait_ge(small_in, 48)

            def bias_dots(s, loaded, value):
                dve.wait_ge(loaded, value)
                for t in range(CT):
                    j = CT * s + t
                    link(v.tensor_tensor_reduce(out=junk, in0=w_qkv[s][:, t, :], in1=beta_row, scale=1.0, scalar=0.0,
                                                op0=ALU.mult, op1=ALU.add, accum_out=bdot[:, j:j + 1]))

            bias_dots(0, wqk_in, 32)
            bias_dots(1, wqk_in, 32)
            link(v.tensor_tensor(bt[:, 0:2 * CT], bdot[:, 0:2 * CT], qkvb[:, 0:2 * CT], ALU.add))
            v.tensor_tensor(prod[:, :], bt[:, 0:CT], bt[:, CT:2 * CT], ALU.mult).then_inc(bias_qk, 1)

            for t in range(CT):
                dve.wait_ge(set_full, t + 1)
                v.scalar_tensor_tensor(out=at32[:, t, :], in0=bank[t % MB][:, :], scalar=gam[:, t:t + 1],
                                       in1=gam_row, op0=ALU.mult, op1=ALU.mult).then_inc(set_evac, 1)
            for t in range(CT):
                dve.wait_ge(set_full, CT + t + 1)
                v.tensor_copy(w_pt[:, t, :], bank[(CT + t) % MB][:, :]).then_inc(set_evac, 1)
            bias_dots(2, wv_in, 16)
            v.tensor_tensor(bt[:, 2 * CT:3 * CT], bdot[:, 2 * CT:3 * CT], qkvb[:, 2 * CT:3 * CT],
                            ALU.add).then_inc(bias_v, 1)
            dve.wait_ge(set_evac, 2 * CT)
            link(v.tensor_reduce(am[:, 0:1], at32, axis=AX.XY, op=ALU.max, apply_absolute_value=True))
            for i in range(2 * CT):
                stats(b0, i)
            dve.wait_ge(stat_step, 1)
            norm_a(b0)
            for t in range(CT):
                dve.wait_ge(set_full, 2 * CT + t + 1)
                v.tensor_scalar(bt32[:, t, :], bank[(2 * CT + t) % MB][:, :], gam[:, t:t + 1], None,
                                ALU.mult).then_inc(set_evac, 1)
            dve.wait_ge(set_evac, 3 * CT)
            link(v.tensor_reduce(am[:, 1:2], bt32, axis=AX.XY, op=ALU.max, apply_absolute_value=True))
            dve.wait_ge(vec_full, 1)
            link(v.tensor_copy(tv[:, 0:3 * CT + 1], ps_small[:, 16:16 + 3 * CT + 1]))
            link(v.tensor_tensor(ta[:, :], tv[:, 0:CT], gam[:, :], ALU.mult))
            link(v.tensor_reduce(am[:, 2:3], ta[:, :], axis=AX.X, op=ALU.max, apply_absolute_value=True))
            v.tensor_tensor(obias[:, :], tv[:, 2 * CT:3 * CT], projb[:, :], ALU.add).then_inc(am_ready, 1)
            norm_b(b0)
            norm_c(b0)
            dve.wait_ge(absmax, 1)
            link(v.tensor_scalar(s0[:, 0:2], amr[:, 0:2], 1e-30, None, ALU.max))
            link(v.scalar_tensor_tensor(out=s0[:, 2:3], in0=s0[:, 0:1], scalar=C * XMAX, in1=amr[:, 2:3],
                                        op0=ALU.mult, op1=ALU.add))
            link(v.reciprocal(s1[:, 0:3], s0[:, 0:3]))
            link(v.tensor_scalar(s0[:, 0:2], s1[:, 0:2], W_TOP, None, ALU.mult))
            link(v.tensor_scalar(s0[:, 2:3], s1[:, 2:3], T_TOP, None, ALU.mult))
            link(v.tensor_single_scalar(sc[:, 0:3].bitcast(i32), s0[:, 0:3].bitcast(i32), 0x7F800000, ALU.bitwise_and))
            link(v.reciprocal(si[:, 0:3], sc[:, 0:3]))
            link(v.tensor_tensor(ft[:, :], sc[:, 2:3], si[:, 0:1], ALU.mult))
            link(v.tensor_scalar(esc[:, :], si[:, 2:3], SCALE, None, ALU.mult))
            link(v.tensor_scalar(cu[:, :], si[:, 1:2], 1.0 / U_SCALE, None, ALU.mult))
            link(v.tensor_scalar(ta[:, :], ta[:, :], sc[:, 2:3], None, ALU.mult))
            link(v.tensor_tensor(gw[:, :], tv[:, CT:2 * CT], gam[:, :], ALU.mult))
            link(v.tensor_scalar(gw[:, :], gw[:, :], sc[:, 2:3], None, ALU.mult))
            v.tensor_scalar(gc[:, :], tv[:, 3 * CT:3 * CT + 1], sc[:, 2:3], None, ALU.mult).then_inc(split_ready, 1)
            for hi, lo, m, j in ((ah, al, at32, 0), (bh, bl, bt32, 1)):
                link(v.tensor_scalar(m, m, sc[:, j:j + 1], None, ALU.mult))
                link(v.tensor_copy(hi[:, :, :], m))
                v.tensor_tensor(lo[:, :, :], m, hi[:, :, :], ALU.subtract).then_inc(scratch_free if j else mat_a, 1)
            for c in range(CT):
                x_low(b0, c)
            for i in range(PER["t"]):
                t_low(b0, i)
            g_columns(b0)
            for i in range(PER["u"]):
                u_low(b0, i, bank[(PER["t"] + i) % MB])

            def one(b, last):
                bn = nxt(b)
                seq = LAST if last else BATCH
                bk = {g: bank[(BASE + n) % MB] for n, g in enumerate(seq)}
                for k in range(NK):
                    max_part(b, 0, k)
                    if not last:
                        stats(bn, 2 * k)
                        stats(bn, 2 * k + 1)
                if not last:
                    wait(dve, stat_step, STATS, bn, 1)
                max_pair(b, 0)
                if not last:
                    norm_a(bn)
                max_all(b, 0)
                if not last:
                    norm_b(bn)
                sub(b, 0, 0)
                sub(b, 0, 1)
                if not last:
                    norm_c(bn)
                sub(b, 0, 2)
                sub(b, 0, 3)
                if not last:
                    for c in range(CT):
                        x_low(bn, c)
                for k in range(NK):
                    max_part(b, 1, k)
                split(b, 0, 0)
                split(b, 0, 1)
                max_pair(b, 1)
                max_all(b, 1)
                for step in ("T0", "T1", "P02", "T2", "P03", "T3", "F", "B0", "B1", "T4", "T5", "B2", "B3",
                             "T6", "T7"):
                    n = int(step[-1]) if len(step) > 1 else 0
                    if step[0] == "T":
                        if not last:
                            t_low(bn, n)
                    elif step[0] == "P":
                        split(b, 0, n)
                    elif step[0] == "B":
                        sub(b, 1, n)
                    else:
                        sum_parts(b, 0)
                if not last:
                    g_columns(bn)
                split(b, 1, 0)
                split(b, 1, 1)
                inverse(b, 0)
                out_group(b, 0, bk["o", 0])
                split(b, 1, 2)
                out_group(b, 1, bk["o", 1])
                split(b, 1, 3)
                sum_parts(b, 1)
                out_group(b, 2, bk["o", 2])
                out_group(b, 3, bk["o", 3])
                inverse(b, 1)
                for c in range(CT):
                    out_group(b, CT + c, bk["o", CT + c])
                if not last:
                    for i in range(PER["u"]):
                        u_low(bn, i, bk["u", i])

            batches(dve, one)

        @block.tensor
        def _(pe):
            mm = nc.tensor.matmul

            def three(dst, parts, n):
                for k in range(n):
                    (wh, wl), (mh, ml) = parts(k)
                    mm(dst, wh, mh, start=(k == 0), stop=False)
                    mm(dst, wh, ml, start=False, stop=False)
                    ins = mm(dst, wl, mh, start=False, stop=(k == n - 1))
                return ins

            def t_group(bn, i, dst):
                ct, mh = i // NH, i % NH
                p = parity(bn)
                if i == 0:
                    wait(pe, xl_done, CT, bn, CT)
                w, m = slice(ct * P, ct * P + P), slice(mh * H, mh * H + H)
                three(dst[:, :], lambda k: ((ah[:, k, w], al[:, k, w]), (xh[p][:, k, m], xl[p][:, k, m])),
                      CT).then_inc(full["t"], 1)

            def u_group(bn, i, dst):
                p = parity(bn)
                w = slice(i * P, i * P + P)
                three(dst[:, :], lambda k: ((xh[p][:, k, w], xl[p][:, k, w]), (bh[:, k, :], bl[:, k, :])),
                      CT).then_inc(full["u"], 1)

            def s_group(b, i, dst):
                h, mt = i // MT, i % MT
                p = parity(b)
                if i == 0:
                    wait(pe, tl_done, PER["t"], b, PER["t"])
                w, n = slice(mt * P, mt * P + P), slice(h * H, h * H + H)
                three(dst[:, :], lambda k: ((th[:, k, w], tl[:, k, w]), (xh[p][:, k, n], xl[p][:, k, n])),
                      CT).then_inc(full["s"], 1)

            def o_group(b, i, dst):
                h, c = i // CT, i % CT
                w = slice(c * P, c * P + P)
                if i == 0:
                    wait(pe, evac["u"], PER["u"], b, PER["u"])
                for mt in range(MT):
                    hi, lo = chunk(h, mt // KC)
                    n = slice((mt % KC) * H, (mt % KC) * H + H)
                    if c == 0 and mt % KC == 0:
                        wait(pe, pl_done, NH * NK, b, NK * h + mt // KC + 1)
                    mm(dst[:, :], uh[:, mt, w], hi[:, n], start=(mt == 0), stop=False)
                    mm(dst[:, :], uh[:, mt, w], lo[:, n], start=False, stop=False)
                    ins = mm(dst[:, :], ul[:, mt, w], hi[:, n], start=False, stop=(mt == MT - 1))
                ins.then_inc(full["o"], 1)

            def g_sums(bn):
                wait(pe, xf_free, CT, bn, CT)
                wait(pe, g_ready, 1, bn, 0)
                for mt in range(MT):
                    ins = mm(ps_g[:, mt:mt + 1], gacc[:, mt * P:mt * P + P], ones[:, 0:1], start=True, stop=True)
                ins.then_inc(g_full, 1)

            def prob_sums(b, h):
                wait(pe, sum_split, NH, b, h + 1)
                wait(pe, rinv_done, NH, b, h)
                mm(ps_sum[:, :], ones16[:, :], sh[:, :], start=True, stop=False)
                mm(ps_sum[:, :], ones16[:, :], sl[:, :], start=False, stop=True).then_inc(sum_full, 1)

            def group_means(bn):
                wait(pe, stat_step, STATS, bn, 2)
                mm(ps_small[:, 0:CT], gmean[:, :], mv[:, :, 0], start=True, stop=True).then_inc(stat_pe, 1)

            def group_vars(bn):
                wait(pe, stat_step, STATS, bn, 6)
                mm(ps_small[:, CT:2 * CT], gmean[:, :], dev[:, :], start=True, stop=True).then_inc(stat_pe, 1)

            b0 = (None, 0)
            pe.wait_ge(consts, 5)
            pe.wait_ge(wqk_in, 32)
            wq, wk, wv = w_qkv
            for t in range(CT):
                for o in range(CT):
                    ins = mm(bank[t][:, :], wk[:, o, t * P:t * P + P], wq[:, o, :], start=(o == 0), stop=(o == CT - 1))
                ins.then_inc(set_full, 1)
            pe.wait_ge(wp_in, 16)
            for t in range(CT):
                g = CT + t
                if g >= MB:
                    pe.wait_ge(set_evac, g - MB + 1)
                for o in range(CT):
                    ins = nc.tensor.transpose(bank[g % MB][:, o * P:o * P + P], w_p[:, o, t * P:t * P + P], ident[:, :])
                ins.then_inc(set_full, 1)
            pe.wait_ge(wv_in, 16)
            pe.wait_ge(set_evac, 2 * CT)
            for t in range(CT):
                for o in range(CT):
                    ins = mm(bank[(2 * CT + t) % MB][:, :], wv[:, o, t * P:t * P + P], w_pt[:, o, :],
                             start=(o == 0), stop=(o == CT - 1))
                ins.then_inc(set_full, 1)
            pe.wait_ge(bias_qk, 1)
            pe.wait_ge(bias_v, 1)
            for j, (w, s) in enumerate(((wq, 1), (wk, 0), (w_pt, 2))):
                for t in range(CT):
                    for o in range(CT):
                        mm(ps_small[:, 16 + CT * j + t:17 + CT * j + t], w[:, o, t * P:t * P + P],
                           bt[:, CT * s + o:CT * s + o + 1], start=(o == 0), stop=(o == CT - 1))
            for o in range(CT):
                ins = mm(ps_small[:, 16 + 3 * CT:17 + 3 * CT], ones[:, :], prod[:, o:o + 1], start=(o == 0), stop=(o == CT - 1))
            ins.then_inc(vec_full, 1)
            pe.wait_ge(am_ready, 1)
            group_means(b0)
            group_vars(b0)

            pe.wait_ge(set_evac, 3 * CT)
            pe.wait_ge(mat_a, 1)
            for g, (kind, i) in enumerate(PROLOGUE):
                if g >= MB:
                    k, j = PROLOGUE[g - MB]
                    pe.wait_ge(evac[k], j + 1)
                if (kind, i) == ("u", 0):
                    g_sums(b0)
                    pe.wait_ge(scratch_free, 1)
                (t_group if kind == "t" else u_group)(b0, i, bank[g % MB])

            def one(b, last):
                bn = nxt(b)
                seq = LAST if last else BATCH
                for n, (kind, i) in enumerate(seq):
                    if n >= MB:
                        k, j = seq[n - MB]
                        if k in "so":
                            wait(pe, evac[k], PER[k], b, j + 1)
                        else:
                            wait(pe, evac[k], PER[k], bn, j + 1)
                    else:
                        k, j = BATCH[n - MB]
                        wait(pe, evac[k], PER[k], b, j + 1)
                    dst = bank[(BASE + n) % MB]
                    if kind == "s":
                        s_group(b, i, dst)
                        if i == MT + 1 and not last:
                            group_means(bn)
                        if i == MT + 3 and not last:
                            group_vars(bn)
                    elif kind == "t":
                        t_group(bn, i, dst)
                        if i == PER["t"] - 1:
                            g_sums(bn)
                    elif kind == "o":
                        o_group(b, i, dst)
                        if i % CT == 0:
                            prob_sums(b, i // CT)
                    else:
                        u_group(bn, i, dst)

            batches(pe, one)


_INS = ["x", "L0_conv_gamma", "L0_conv_beta", "L0_conv_qkv_w", "L0_conv_qkv_b", "L0_conv_proj_w", "L0_conv_proj_b"]


def kernel(**inputs):
    import numpy as _np
    import concourse.bacc as _bacc
    from concourse import mybir as _mybir
    from concourse.bass_utils import run_bass_kernel_spmd as _run

    nc = _bacc.Bacc("TRN2", target_bir_lowering=False, num_devices=1)
    arrays, args = {}, []
    for name in _INS:
        a = _np.ascontiguousarray(inputs[name])
        arrays[f"in_{name}"] = a
        args.append(nc.dram_tensor(f"in_{name}", a.shape, _mybir.dt.from_np(a.dtype), kind="ExternalInput").ap())
    shape = arrays["in_x"].shape
    args.append(nc.dram_tensor("out_0", shape, _mybir.dt.float32, kind="ExternalOutput").ap())
    attention_block_kernel(nc, *args)
    r = _run(nc, [arrays], core_ids=[0])
    return r.results[0]["out_0"]
```

```python
import math
from contextlib import ExitStack

import concourse.bass as bass
from concourse import mybir


def attention_block_kernel(nc, x, gamma, beta, qkv_w, qkv_b, proj_w, proj_b, out):
    fp32, fp16, i32 = mybir.dt.float32, mybir.dt.float16, mybir.dt.int32
    ALU, ACT, AX = mybir.AluOpType, mybir.ActivationFunctionType, mybir.AxisListType

    P = 128
    NB, C, HH, WW = x.shape
    N = HH * WW
    GROUP = C // 32
    EPS = 1e-5
    CT, MT = C // P, N // P
    H = 512
    NH = N // H
    KC = 2
    NK = MT // KC
    Q = 32
    SCALE = 1.0 / math.sqrt(C)
    XMAX = 128.0
    W_TOP = 2.0 ** 14
    T_TOP = 2.0 ** 15
    MAXES = 9
    SUMS = 10
    NEWTON = 4
    STATS = 9 + 3 * NEWTON
    U_SCALE = T_TOP / (C * XMAX * W_TOP)
    P_LOG = 12 * math.log(2.0)

    MB = 5
    BATCH = ([("s", i) for i in range(NH * MT)] + [("t", i) for i in range(CT * NH)]
             + [("o", i) for i in range(NH * CT)] + [("u", i) for i in range(MT)])
    LAST = [g for g in BATCH if g[0] in "so"]
    PROLOGUE = [g for g in BATCH if g[0] in "tu"]
    PER = {"s": NH * MT, "t": CT * NH, "o": NH * CT, "u": MT}
    assert len(BATCH) % MB == 0
    BASE = len(PROLOGUE) % MB

    x_d = x.rearrange("b (t p) h w -> b p t (h w)", p=P)
    out_d = out.rearrange("b (t p) h w -> b p t (h w)", p=P)

    ctx = ExitStack()
    with ctx:
        def sb(name, shape, dt=fp32):
            return ctx.enter_context(nc.sbuf_tensor(name, shape, dt))

        def pb(name):
            return ctx.enter_context(nc.psum_tensor(name, [P, 512], fp32))

        def sem(name):
            return ctx.enter_context(nc.semaphore(name))

        xs = [sb(f"x{p}", [P, CT, N]) for p in range(2)]
        xh = [sb(f"xh{p}", [P, CT, N], fp16) for p in range(2)]
        xl = [sb(f"xl{p}", [P, CT, N], fp16) for p in range(2)]
        xf = sb("xf", [P, 2, N])
        th = sb("th", [P, CT, N], fp16)
        tl = sb("tl", [P, CT, N], fp16)
        tf = sb("tf", [P, 4, H])
        uh = sb("uh", [P, MT, C], fp16)
        ul = sb("ul", [P, MT, C], fp16)
        sp = [sb(f"sp{h}", [P, MT, H]) for h in range(NH)]
        pf = sb("pf", [P, 2, KC, H])
        ah = sb("ah", [P, CT, C], fp16)
        al = sb("al", [P, CT, C], fp16)
        bh = sb("bh", [P, CT, C], fp16)
        bl = sb("bl", [P, CT, C], fp16)
        ob = sb("ob", [P, CT, H])
        mx = sb("mx", [P, 2, H])
        tr = sb("tr", [P, H])
        maxb = sb("maxb", [P, H])
        ps2 = sb("ps2", [P, KC, H])
        rinv = [sb(f"rinv{h}", [P, H]) for h in range(NH)]
        gacc = sb("gacc", [P, N])
        gcol = sb("gcol", [P, MT])
        gq = sb("gq", [P, N // Q])
        gg = sb("gg", [P, P // Q, MT])
        gs = sb("gs", [P, MT])
        st = sb("st", [P, CT, 2, 6])
        mv = sb("mv", [P, CT, 2])
        dev = sb("dev", [P, CT])
        var = sb("var", [P, CT])
        rs = sb("rs", [P, CT])
        nt = sb("nt", [P, CT])
        mg = sb("mg", [P, CT])
        nb = sb("nb", [P, CT])
        rq = sb("rq", [P, H // Q])
        rg = sb("rg", [Q, P // Q, H // Q])
        r1 = sb("r1", [Q, H // Q])
        mb = sb("mb", [P, H // Q])
        ident = sb("ident", [P, P])
        gmean = sb("gmean", [P, P])
        ones = sb("ones", [P, P])
        ebias = sb("ebias", [P, 1])
        gam = sb("gam", [P, CT])
        qkvb = sb("qkvb", [P, 3 * CT])
        projb = sb("projb", [P, CT])
        bdot = sb("bdot", [P, 3 * CT])
        bt = sb("bt", [P, 3 * CT])
        prod = sb("prod", [P, CT])
        prod1 = sb("prod1", [P, 1])
        tmax = sb("tmax", [P, CT])
        am = sb("am", [P, 2])
        amr = sb("amr", [P, 2])
        bm = sb("bm", [P, 1])
        bmr = sb("bmr", [P, 1])
        s0 = sb("s0", [P, 3])
        s1 = sb("s1", [P, 3])
        sc = sb("sc", [P, 3])
        si = sb("si", [P, 3])
        ft = sb("ft", [P, 1])
        esc = sb("esc", [P, 1])
        cu = sb("cu", [P, 1])
        ta = sb("ta", [P, CT])
        gw = sb("gw", [P, CT])
        gc = sb("gc", [P, 1])
        obias = sb("obias", [P, CT])
        w_qkv = [sp[0][:, 0:CT, :], sp[0][:, CT:2 * CT, :], sp[1][:, 0:CT, :]]
        w_p = sp[1][:, CT:2 * CT, :]
        w_pt = pf[:, :, :, :].rearrange("p a b n -> p (a b) n")
        at32 = xs[1][:, 0:2, :].rearrange("p a (b n) -> p (a b) n", n=C)
        bt32 = xs[1][:, 2:4, :].rearrange("p a (b n) -> p (a b) n", n=C)
        gam_row, beta_row, junk = maxb[:, :], rinv[0][:, :], rinv[1][:, :]
        vec = gacc[:, :].rearrange("p (a n) -> p a n", a=2)
        vec_o = ps2[:, 0, :]

        bank = [pb(f"bank{i}") for i in range(MB)]
        ps_small, ps_va, ps_vb = pb("ps_small"), pb("ps_va"), pb("ps_vb")

        small_in, wqk_in, wp_in, wv_in = sem("small_in"), sem("wqk_in"), sem("wp_in"), sem("wv_in")
        x_in = [sem("x_in0"), sem("x_in1")]
        masks, consts, row_in = sem("masks"), sem("consts"), sem("row_in")
        set_full, set_step, scratch_free = sem("set_full"), sem("set_step"), sem("scratch_free")
        at_read, wpt_read, bt_read = sem("at_read"), sem("wpt_read"), sem("bt_read")
        vec_ready, vec_full, vo_ready, vo_full = sem("vec_ready"), sem("vec_full"), sem("vo_ready"), sem("vo_full")
        am_ready, absmax, bm_ready, bsmax = sem("am_ready"), sem("absmax"), sem("bm_ready"), sem("bsmax")
        a_scale, b_scale, ah_done, bh_done, a_split = (
            sem("a_scale"), sem("b_scale"), sem("ah_done"), sem("bh_done"), sem("a_split"))
        full = {k: sem(f"{k}_full") for k in "stou"}
        evac = {k: sem(f"{k}_evac") for k in "stou"}
        stat_step, stat_pe = sem("stat_step"), sem("stat_pe")
        rs_ready, xf_done, xh_done, xl_done = sem("rs_ready"), sem("xf_done"), sem("xh_done"), sem("xl_done")
        xf_free, g_step, g_ready = sem("xf_free"), sem("g_step"), sem("g_ready")
        tf_done, tl_done, uh_done = sem("tf_done"), sem("tl_done"), sem("uh_done")
        max_step, max_ready, sub_done = sem("max_step"), sem("max_ready"), sem("sub_done")
        pf_done, ph_done, pl_done = sem("pf_done"), sem("ph_done"), sem("pl_done")
        sum_step, rinv_done = sem("sum_step"), sem("rinv_done")
        out_ready, stored = sem("out_ready"), sem("stored")

        def count(per, batch, off):
            reg, c = batch
            return per * c + off if reg is None else reg * per + (per * c + off)

        def wait(eng, s, per, batch, off):
            reg, c = batch
            if reg is None:
                if per * c + off > 0:
                    eng.wait_ge(s, per * c + off)
            else:
                assert per * (c + 1) + off > 0
                eng.wait_ge(s, count(per, batch, off))

        def parity(batch):
            reg, c = batch
            return c % 2 if reg is None else (c + 1) % 2

        def nxt(batch):
            return batch[0], batch[1] + 1

        def chunk(h, k):
            v = sp[h][:, KC * k:KC * k + KC, :].bitcast(fp16).rearrange("p a n -> p (a n)")
            return v[:, 0:KC * H], v[:, KC * H:2 * KC * H]

        def batches(eng, one):
            one((None, 0), False)
            with eng.Fori(1, NB - 2, 2) as r:
                one((r, 0), False)
                one((r, 1), False)
            one((None, NB - 1), True)

        block = ctx.enter_context(nc.Block())

        @block.sync
        def _(sp_eng):
            wv = qkv_w.rearrange("(s t p) c -> s p t c", s=3, p=P)
            sp_eng.dma_start(w_qkv[0], wv[0]).then_inc(wqk_in, 16)
            sp_eng.dma_start(w_qkv[1], wv[1]).then_inc(wqk_in, 16)
            sp_eng.dma_start(xs[0][:, :, :], x_d[0]).then_inc(x_in[0], 16)
            sp_eng.dma_start(w_p, proj_w.rearrange("(t p) c -> p t c", p=P)).then_inc(wp_in, 16)
            sp_eng.dma_start(w_qkv[2], wv[2]).then_inc(wv_in, 16)

            def one(b, last):
                if not last:
                    nxt_b = nxt(b)
                    if b[0] is None and b[1] == 0:
                        sp_eng.wait_ge(scratch_free, 1)
                    wait(sp_eng, out_ready, PER["o"], b, 0)
                    src = x_d[1] if b[0] is None else x_d[b[0] + nxt_b[1]]
                    sp_eng.dma_start(xs[parity(nxt_b)][:, :, :], src).then_inc(x_in[parity(nxt_b)], 16)
                for h in range(NH):
                    wait(sp_eng, out_ready, PER["o"], b, CT * (h + 1))
                    dst = out_d[b[1]] if b[0] is None else out_d[b[0] + b[1]]
                    sp_eng.dma_start(dst[:, :, h * H:(h + 1) * H], ob[:, :, :]).then_inc(stored, 16)

            batches(sp_eng, one)
            sp_eng.wait_ge(stored, 16 * NH * NB)

        @block.gpsimd
        def _(pool):
            nc.gpsimd.memset(ident[:, :], 0.0).then_inc(masks, 1)
            nc.gpsimd.memset(gmean[:, :], 1.0 / GROUP).then_inc(masks, 1)
            nc.gpsimd.memset(ones[:, :], 1.0).then_inc(consts, 1)
            nc.gpsimd.memset(ebias[:, :], P_LOG).then_inc(consts, 1)
            pool.wait_ge(masks, 2)
            nc.gpsimd.affine_select(out=ident[:, :], in_=ident[:, :], compare_op=ALU.not_equal, fill=1.0,
                                    base=0, pattern=[[-1, P]], channel_multiplier=1).then_inc(consts, 1)
            blocks = gmean[:, :].rearrange("p (g j) -> p g j", j=GROUP)
            nc.gpsimd.affine_select(out=blocks, in_=blocks, compare_op=ALU.is_ge, fill=0.0, base=0,
                                    pattern=[[-GROUP, P // GROUP], [0, GROUP]], channel_multiplier=1).then_inc(masks, 1)
            pool.wait_ge(masks, 3)
            nc.gpsimd.affine_select(out=blocks, in_=blocks, compare_op=ALU.is_ge, fill=0.0, base=GROUP - 1,
                                    pattern=[[GROUP, P // GROUP], [0, GROUP]], channel_multiplier=-1).then_inc(consts, 1)
            pool.wait_ge(am_ready, 1)
            nc.gpsimd.partition_all_reduce(amr[:, :], am[:, :], P, bass.bass_isa.ReduceOp.absmax).then_inc(absmax, 1)
            pool.wait_ge(bm_ready, 1)
            nc.gpsimd.partition_all_reduce(bmr[:, :], bm[:, :], P, bass.bass_isa.ReduceOp.absmax).then_inc(bsmax, 1)

        @block.scalar
        def _(act):
            act.dma_start(beta_row, beta.partition_broadcast(P)).then_inc(row_in, 16)
            act.dma_start(gam_row, gamma.partition_broadcast(P)).then_inc(row_in, 16)
            with nc.allow_non_contiguous_dma(reason="biases, a value per partition"):
                act.dma_start(gam[:, :], gamma.rearrange("(t p) -> p t", p=P)).then_inc(small_in, 16)
                act.dma_start(qkvb[:, :], qkv_b.rearrange("(t p) -> p t", p=P)).then_inc(small_in, 16)
                act.dma_start(projb[:, :], proj_b.rearrange("(t p) -> p t", p=P)).then_inc(small_in, 16)

            def x_norm(bn, c):
                p = parity(bn)
                wait(act, rs_ready, 1, bn, 1)
                wait(act, xf_free, CT, bn, c - 1)
                nc.scalar.activation(xf[:, c % 2, :], xs[p][:, c, :], ACT.Identity,
                                     bias=nb[:, c:c + 1], scale=rs[:, c:c + 1]).then_inc(xf_done, 1)
                nc.scalar.activation(xh[p][:, c, :], xs[p][:, c, :], ACT.Identity,
                                     bias=nb[:, c:c + 1], scale=rs[:, c:c + 1]).then_inc(xh_done, 1)

            def t_group(bn, i, bk):
                ct, mh = i // NH, i % NH
                wait(act, full["t"], PER["t"], bn, i + 1)
                wait(act, tl_done, PER["t"], bn, i - 3)
                nc.scalar.activation(tf[:, i % 4, :], bk[:, :], ACT.Identity,
                                     bias=ta[:, ct:ct + 1], scale=ft[:, 0:1]).then_inc(tf_done, 1)
                nc.scalar.activation(th[:, ct, mh * H:(mh + 1) * H], bk[:, :], ACT.Identity,
                                     bias=ta[:, ct:ct + 1], scale=ft[:, 0:1]).then_inc(evac["t"], 1)

            def u_group(bn, i, bk):
                wait(act, full["u"], PER["u"], bn, i + 1)
                nc.scalar.activation(uh[:, i, :], bk[:, :], ACT.Copy, scale=U_SCALE).then_inc(uh_done, 1)

            def s_group(b, i, bk):
                h, mt = i // MT, i % MT
                wait(act, full["s"], PER["s"], b, i + 1)
                if i == 0:
                    wait(act, g_ready, 1, b, 1)
                if mt == 0:
                    wait(act, full["o"], PER["o"], b, CT * (h + 1) - PER["o"])
                nc.scalar.activation(sp[h][:, mt, :], bk[:, :], ACT.Identity,
                                     bias=gcol[:, mt:mt + 1]).then_inc(evac["s"], 1)

            def exps(b, h, k):
                n = NK * h + k
                wait(act, sub_done, NH * NK, b, n + 1)
                wait(act, sum_step, NH * SUMS, b, SUMS * h + (1 if k >= 2 else k + 2 - SUMS))
                nc.scalar.activation(pf[:, k % 2, :, :], sp[h][:, KC * k:KC * k + KC, :], ACT.Exp,
                                     bias=ebias[:, 0:1], scale=esc[:, 0:1]).then_inc(pf_done, 1)

            def high(b, h, k):
                wait(act, pf_done, NH * NK, b, NK * h + k + 1)
                hi, _ = chunk(h, k)
                nc.scalar.activation(hi, pf[:, k % 2, :, :].rearrange("p a n -> p (a n)"), ACT.Copy).then_inc(ph_done, 1)

            b0 = (None, 0)
            act.wait_ge(consts, 4)
            act.wait_ge(small_in, 48)
            for t in range(CT):
                act.wait_ge(set_full, CT + t + 1)
                nc.scalar.activation(w_pt[:, t, :], bank[(CT + t) % MB][:, :], ACT.Copy).then_inc(wpt_read, 1)
            act.wait_ge(a_scale, 1)
            nc.scalar.activation(ah[:, :, :], at32, ACT.Copy, scale=sc[:, 0:1]).then_inc(ah_done, 1)
            for c in range(CT):
                x_norm(b0, c)
            for t in range(CT):
                act.wait_ge(set_full, 2 * CT + t + 1)
                nc.scalar.activation(bt32[:, t, :], bank[(2 * CT + t) % MB][:, :], ACT.Copy,
                                     scale=gam[:, t:t + 1]).then_inc(bt_read, 1)
            for i in range(CT):
                t_group(b0, i, bank[i % MB])
            act.wait_ge(b_scale, 1)
            nc.scalar.activation(bh[:, :, :], bt32, ACT.Copy, scale=sc[:, 2:3]).then_inc(bh_done, 1)
            for i in range(CT, PER["t"]):
                t_group(b0, i, bank[i % MB])
            for i in range(PER["u"]):
                u_group(b0, i, bank[(PER["t"] + i) % MB])

            def one(b, last):
                bn = nxt(b)
                seq = LAST if last else BATCH
                bk = {g: bank[(BASE + n) % MB] for n, g in enumerate(seq)}
                for i in range(MT):
                    s_group(b, i, bk["s", i])
                s1_order = ["X0", "S0", "X1", "S1", "E0", "S2", "E1", "X2", "S3", "S4", "X3", "S5", "S6", "S7"]
                for step in s1_order:
                    n = int(step[1])
                    if step[0] == "S":
                        s_group(b, MT + n, bk["s", MT + n])
                    elif step[0] == "E":
                        exps(b, 0, n)
                    elif not last:
                        x_norm(bn, n)
                t_order = ["H00", "H01", "T0", "E02", "T1", "E03", "H02", "T2", "H03", "T3", "T4",
                           "E10", "T5", "E11", "T6", "H10", "T7", "H11", "E12", "H12", "E13", "H13"]
                for step in t_order:
                    if step[0] == "T":
                        if not last:
                            t_group(bn, int(step[1]), bk["t", int(step[1])])
                    else:
                        (exps if step[0] == "E" else high)(b, int(step[1]), int(step[2]))
                if not last:
                    for i in range(MT):
                        u_group(bn, i, bk["u", i])

            batches(act, one)

        @block.vector
        def _(dve):
            v = nc.vector
            steps = [0]

            def link(ins):
                steps[0] += 1
                ins.then_inc(set_step, 1)
                dve.wait_ge(set_step, steps[0])

            def stats(bn, i):
                p = parity(bn)
                if i == 0:
                    wait(dve, x_in[p], 8, bn, 16 - 8 * p)
                ins = v.bn_stats(st[:, i // 2, i % 2, :], xs[p][:, i // 2, (i % 2) * 512:(i % 2 + 1) * 512])
                if i == 2 * CT - 1:
                    ins.then_inc(stat_step, 1)

            def norm_a(bn):
                for c in range(CT):
                    ins = v.bn_aggr(mv[:, c, :], st[:, c, :, :].rearrange("p a b -> p (a b)"))
                ins.then_inc(stat_step, 1)

            def norm_b(bn):
                wait(dve, stat_pe, 2, bn, 1)
                v.tensor_copy(mg[:, :], ps_small[:, 0:CT]).then_inc(stat_step, 1)
                wait(dve, stat_step, STATS, bn, 3)
                v.tensor_tensor(dev[:, :], mv[:, :, 0], mg[:, :], ALU.subtract).then_inc(stat_step, 1)
                wait(dve, stat_step, STATS, bn, 4)
                v.tensor_tensor(var[:, :], dev[:, :], dev[:, :], ALU.mult).then_inc(stat_step, 1)
                wait(dve, stat_step, STATS, bn, 5)
                v.tensor_tensor(dev[:, :], var[:, :], mv[:, :, 1], ALU.add).then_inc(stat_step, 1)

            def norm_c(bn):
                wait(dve, stat_pe, 2, bn, 2)
                v.tensor_scalar(var[:, :], ps_small[:, CT:2 * CT], EPS, None, ALU.add).then_inc(stat_step, 1)
                wait(dve, stat_step, STATS, bn, 7)
                v.tensor_single_scalar(nt[:, :].bitcast(i32), var[:, :].bitcast(i32), 1,
                                       ALU.logical_shift_right).then_inc(stat_step, 1)
                wait(dve, stat_step, STATS, bn, 8)
                v.tensor_scalar(rs[:, :].bitcast(i32), nt[:, :].bitcast(i32), -1.0, float(0x5F3759DF),
                                ALU.mult, ALU.add).then_inc(stat_step, 1)
                for k in range(NEWTON):
                    wait(dve, stat_step, STATS, bn, 9 + 3 * k)
                    v.tensor_tensor(nt[:, :], rs[:, :], rs[:, :], ALU.mult).then_inc(stat_step, 1)
                    wait(dve, stat_step, STATS, bn, 10 + 3 * k)
                    v.scalar_tensor_tensor(out=dev[:, :], in0=nt[:, :], scalar=-0.5, in1=var[:, :],
                                           op0=ALU.mult, op1=ALU.mult).then_inc(stat_step, 1)
                    wait(dve, stat_step, STATS, bn, 11 + 3 * k)
                    v.scalar_tensor_tensor(out=rs[:, :], in0=dev[:, :], scalar=1.5, in1=rs[:, :],
                                           op0=ALU.add, op1=ALU.mult).then_inc(stat_step, 1)
                wait(dve, stat_step, STATS, bn, STATS)
                v.scalar_tensor_tensor(out=nb[:, :], in0=mg[:, :], scalar=-1.0, in1=rs[:, :],
                                       op0=ALU.mult, op1=ALU.mult).then_inc(rs_ready, 1)

            def x_low(bn, c):
                p = parity(bn)
                wait(dve, xf_done, CT, bn, c + 1)
                wait(dve, xh_done, CT, bn, c + 1)
                v.tensor_tensor(xl[p][:, c, :], xf[:, c % 2, :], xh[p][:, c, :], ALU.subtract).then_inc(xl_done, 1)
                if c == 0:
                    v.tensor_scalar(gacc[:, :], xf[:, 0, :], gw[:, 0:1], None, ALU.mult).then_inc(xf_free, 1)
                else:
                    wait(dve, xf_free, CT, bn, c)
                    v.scalar_tensor_tensor(out=gacc[:, :], in0=xf[:, c % 2, :], scalar=gw[:, c:c + 1],
                                           in1=gacc[:, :], op0=ALU.mult, op1=ALU.add).then_inc(xf_free, 1)

            def g_columns(bn):
                wait(dve, xf_free, CT, bn, CT)
                flat = mx[:, :, :].rearrange("p a n -> p (a n)")
                v.transpose(flat, gacc[:, :]).then_inc(g_step, 1)
                wait(dve, g_step, 4, bn, 1)
                v.tensor_reduce(gq[:, :], flat.rearrange("p (k i) -> p k i", i=Q), axis=AX.X,
                                op=ALU.add).then_inc(g_step, 1)
                wait(dve, g_step, 4, bn, 2)
                for a in range(P // Q):
                    for q in range(P // Q):
                        ins = v.tensor_copy(gg[Q * a:Q * a + Q, q, :], gq[Q * q:Q * q + Q, a:N // Q:P // Q])
                ins.then_inc(g_step, 1)
                wait(dve, g_step, 4, bn, 3)
                v.tensor_reduce(gs[:, :], gg[:, :, :].rearrange("p q m -> p m q"), axis=AX.X,
                                op=ALU.add).then_inc(g_step, 1)
                wait(dve, g_step, 4, bn, 4)
                v.tensor_scalar(gcol[:, :], gs[:, :], gc[:, 0:1], None, ALU.add).then_inc(g_ready, 1)

            def t_low(bn, i):
                ct, mh = i // NH, i % NH
                wait(dve, tf_done, PER["t"], bn, i + 1)
                wait(dve, evac["t"], PER["t"], bn, i + 1)
                v.tensor_tensor(tl[:, ct, mh * H:(mh + 1) * H], tf[:, i % 4, :], th[:, ct, mh * H:(mh + 1) * H],
                                ALU.subtract).then_inc(tl_done, 1)

            def u_low(bn, i, bk):
                wait(dve, uh_done, PER["u"], bn, i + 1)
                v.scalar_tensor_tensor(out=ul[:, i, :], in0=bk[:, :], scalar=U_SCALE, in1=uh[:, i, :],
                                       op0=ALU.mult, op1=ALU.subtract).then_inc(evac["u"], 1)

            def max_part(b, h, k):
                if k == 0:
                    return
                a, c = NH * MAXES, MAXES * h
                wait(dve, evac["s"], PER["s"], b, MT * h + KC * (k + 1))
                if k >= 2:
                    wait(dve, max_step, a, b, c + k - 1)
                first = sp[h][:, 0:KC, :] if k == 1 else mx[:, :, :]
                v.tensor_tensor(mx[:, :, :], first, sp[h][:, KC * k:KC * k + KC, :], ALU.max).then_inc(max_step, 1)

            def max_pair(b, h):
                wait(dve, max_step, NH * MAXES, b, MAXES * h + 3)
                v.tensor_tensor(mx[:, 0, :], mx[:, 0, :], mx[:, 1, :], ALU.max).then_inc(max_step, 1)

            def across(src, dst, op, b, step, per, c, done, invert=False):
                wait(dve, step, per, b, c)
                v.transpose(tr[:, :], src).then_inc(step, 1)
                wait(dve, step, per, b, c + 1)
                v.tensor_reduce(rq[:, :], tr[:, :].rearrange("p (k i) -> p k i", i=Q), axis=AX.X, op=op).then_inc(step, 1)
                wait(dve, step, per, b, c + 2)
                for q in range(P // Q):
                    ins = v.tensor_copy(rg[:, q, :], rq[Q * q:Q * q + Q, :])
                ins.then_inc(step, 1)
                wait(dve, step, per, b, c + 3)
                v.tensor_reduce(r1[:, :], rg[:, :, :].rearrange("p q k -> p k q"), axis=AX.X, op=op).then_inc(step, 1)
                wait(dve, step, per, b, c + 4)
                if invert:
                    v.reciprocal(r1[:, :], r1[:, :]).then_inc(step, 1)
                    c += 1
                    wait(dve, step, per, b, c + 4)
                for q in range(P // Q):
                    ins = v.tensor_copy(mb[Q * q:Q * q + Q, :], r1[:, :])
                ins.then_inc(step, 1)
                wait(dve, step, per, b, c + 5)
                v.transpose(dst.rearrange("p (k i) -> p k i", i=Q),
                            mb[:, :].unsqueeze(2).to_broadcast([P, H // Q, Q])).then_inc(done, 1)

            def max_all(b, h):
                across(mx[:, 0, :], maxb[:, :], ALU.max, b, max_step, NH * MAXES, MAXES * h + 4, max_ready)

            def sub(b, h, k):
                if k == 0:
                    wait(dve, max_ready, NH, b, h + 1)
                tile = sp[h][:, KC * k:KC * k + KC, :]
                v.tensor_tensor(tile, tile, maxb[:, :].unsqueeze(1).to_broadcast([P, KC, H]),
                                ALU.subtract).then_inc(sub_done, 1)

            def split(b, h, k):
                a, c = NH * SUMS, SUMS * h
                wait(dve, ph_done, NH * NK, b, NK * h + k + 1)
                hi, lo = chunk(h, k)
                v.tensor_tensor(lo, pf[:, k % 2, :, :].rearrange("p a n -> p (a n)"), hi, ALU.subtract).then_inc(pl_done, 1)
                if k == 1:
                    v.tensor_tensor(ps2[:, :, :], pf[:, 0, :, :], pf[:, 1, :, :], ALU.add).then_inc(sum_step, 1)
                elif k >= 2:
                    wait(dve, sum_step, a, b, c + k - 1)
                    v.tensor_tensor(ps2[:, :, :], ps2[:, :, :], pf[:, k % 2, :, :], ALU.add).then_inc(sum_step, 1)

            def inverse(b, h):
                wait(dve, sum_step, NH * SUMS, b, SUMS * h + 3)
                v.tensor_tensor(ps2[:, 0, :], ps2[:, 0, :], ps2[:, 1, :], ALU.add).then_inc(sum_step, 1)
                across(ps2[:, 0, :], rinv[h][:, :], ALU.add, b, sum_step, NH * SUMS, SUMS * h + 4, rinv_done, invert=True)

            def out_group(b, i, bk):
                h, c = i // CT, i % CT
                wait(dve, full["o"], PER["o"], b, i + 1)
                if c == 0:
                    wait(dve, rinv_done, NH, b, h + 1)
                    wait(dve, stored, 16 * NH, b, 16 * h)
                v.scalar_tensor_tensor(out=ob[:, c, :], in0=bk[:, :], scalar=cu[:, 0:1], in1=rinv[h][:, :],
                                       op0=ALU.mult, op1=ALU.mult).then_inc(evac["o"], 1)
                wait(dve, evac["o"], PER["o"], b, i + 1)
                v.scalar_tensor_tensor(out=ob[:, c, :], in0=ob[:, c, :], scalar=obias[:, c:c + 1],
                                       in1=xs[parity(b)][:, c, h * H:(h + 1) * H],
                                       op0=ALU.add, op1=ALU.add).then_inc(out_ready, 1)

            b0 = (None, 0)

            def bias_dots(s):
                for t in range(CT):
                    j = CT * s + t
                    link(v.tensor_tensor_reduce(out=junk, in0=w_qkv[s][:, t, :], in1=beta_row, scale=1.0, scalar=0.0,
                                                op0=ALU.mult, op1=ALU.add, accum_out=bdot[:, j:j + 1]))
                r = slice(CT * s, CT * s + CT)
                link(v.tensor_tensor(bt[:, r], bdot[:, r], qkvb[:, r], ALU.add))

            def tile_sums(dst, w, s, done):
                link(v.tensor_scalar(dst, w[:, 0, :], bt[:, CT * s:CT * s + 1], None, ALU.mult))
                for o in range(1, CT):
                    ins = v.scalar_tensor_tensor(out=dst, in0=w[:, o, :], scalar=bt[:, CT * s + o:CT * s + o + 1],
                                                 in1=dst, op0=ALU.mult, op1=ALU.add)
                    if o < CT - 1:
                        link(ins)
                ins.then_inc(done, 1)

            def powers(dst, src, top):
                link(v.reciprocal(s1[:, dst], src))
                link(v.tensor_scalar(s0[:, dst], s1[:, dst], top, None, ALU.mult))
                link(v.tensor_single_scalar(sc[:, dst].bitcast(i32), s0[:, dst].bitcast(i32), 0x7F800000, ALU.bitwise_and))
                link(v.reciprocal(si[:, dst], sc[:, dst]))

            dve.wait_ge(row_in, 32)
            dve.wait_ge(small_in, 48)
            dve.wait_ge(wqk_in, 32)
            bias_dots(1)
            tile_sums(vec[:, 0, :], w_qkv[0], 1, vec_ready)
            bias_dots(0)
            tile_sums(vec[:, 1, :], w_qkv[1], 0, vec_ready)
            link(v.tensor_tensor(prod[:, :], bt[:, 0:CT], bt[:, CT:2 * CT], ALU.mult))
            v.tensor_reduce(prod1[:, :], prod[:, :], axis=AX.X, op=ALU.add).then_inc(vec_ready, 1)
            for t in range(CT):
                dve.wait_ge(set_full, t + 1)
                v.scalar_tensor_tensor(out=at32[:, t, :], in0=bank[t % MB][:, :], scalar=gam[:, t:t + 1],
                                       in1=gam_row, op0=ALU.mult, op1=ALU.mult).then_inc(at_read, 1)
                dve.wait_ge(at_read, t + 1)
                link(v.tensor_reduce(tmax[:, t:t + 1], at32[:, t, :], axis=AX.X, op=ALU.max, apply_absolute_value=True))
            dve.wait_ge(vec_full, 1)
            link(v.tensor_tensor(ta[:, :], ps_va[:, 0:CT], gam[:, :], ALU.mult))
            link(v.tensor_tensor(gw[:, :], ps_va[:, CT:2 * CT], gam[:, :], ALU.mult))
            link(v.tensor_copy(gc[:, :], ps_va[:, 2 * CT:2 * CT + 1]))
            link(v.tensor_reduce(am[:, 0:1], tmax[:, :], axis=AX.X, op=ALU.max))
            v.tensor_reduce(am[:, 1:2], ta[:, :], axis=AX.X, op=ALU.max, apply_absolute_value=True).then_inc(am_ready, 1)
            for i in range(2 * CT):
                stats(b0, i)
            dve.wait_ge(stat_step, 1)
            norm_a(b0)
            dve.wait_ge(absmax, 1)
            link(v.tensor_scalar(s0[:, 0:1], amr[:, 0:1], 1e-30, None, ALU.max))
            powers(slice(0, 1), s0[:, 0:1], W_TOP)
            link(v.tensor_scalar(s1[:, 2:3], amr[:, 0:1], 1e-30, None, ALU.max))
            link(v.scalar_tensor_tensor(out=s0[:, 1:2], in0=s1[:, 2:3], scalar=C * XMAX, in1=amr[:, 1:2],
                                        op0=ALU.mult, op1=ALU.add))
            powers(slice(1, 2), s0[:, 1:2], T_TOP)
            v.tensor_tensor(ft[:, :], sc[:, 1:2], si[:, 0:1], ALU.mult).then_inc(a_scale, 1)
            norm_b(b0)
            norm_c(b0)
            link(v.tensor_scalar(esc[:, :], si[:, 1:2], SCALE, None, ALU.mult))
            link(v.tensor_scalar(ta[:, :], ta[:, :], sc[:, 1:2], None, ALU.mult))
            link(v.tensor_scalar(gw[:, :], gw[:, :], sc[:, 1:2], None, ALU.mult))
            link(v.tensor_scalar(gc[:, :], gc[:, :], sc[:, 1:2], None, ALU.mult))
            dve.wait_ge(ah_done, 1)
            v.scalar_tensor_tensor(out=al[:, :, :], in0=at32, scalar=sc[:, 0:1], in1=ah[:, :, :],
                                   op0=ALU.mult, op1=ALU.subtract).then_inc(a_split, 1)
            for c in range(CT):
                x_low(b0, c)
            dve.wait_ge(wv_in, 16)
            bias_dots(2)
            tile_sums(vec_o, w_pt, 2, vo_ready)
            dve.wait_ge(bt_read, CT)
            v.tensor_reduce(bm[:, :], bt32, axis=AX.XY, op=ALU.max, apply_absolute_value=True).then_inc(bm_ready, 1)
            t_low(b0, 0)
            t_low(b0, 1)
            dve.wait_ge(bsmax, 1)
            link(v.tensor_scalar(s0[:, 2:3], bmr[:, :], 1e-30, None, ALU.max))
            powers(slice(2, 3), s0[:, 2:3], W_TOP)
            v.tensor_scalar(cu[:, :], si[:, 2:3], 1.0 / U_SCALE, None, ALU.mult).then_inc(b_scale, 1)
            t_low(b0, 2)
            t_low(b0, 3)
            dve.wait_ge(bh_done, 1)
            v.scalar_tensor_tensor(out=bl[:, :, :], in0=bt32, scalar=sc[:, 2:3], in1=bh[:, :, :],
                                   op0=ALU.mult, op1=ALU.subtract).then_inc(scratch_free, 1)
            for i in range(4, PER["t"]):
                t_low(b0, i)
            dve.wait_ge(vo_full, 1)
            v.tensor_tensor(obias[:, :], ps_vb[:, 0:CT], projb[:, :], ALU.add)
            g_columns(b0)
            for i in range(PER["u"]):
                u_low(b0, i, bank[(PER["t"] + i) % MB])

            def one(b, last):
                bn = nxt(b)
                seq = LAST if last else BATCH
                bk = {g: bank[(BASE + n) % MB] for n, g in enumerate(seq)}
                if not last:
                    for i in range(2 * CT):
                        stats(bn, i)
                    wait(dve, stat_step, STATS, bn, 1)
                max_part(b, 0, 1)
                if not last:
                    norm_a(bn)
                    norm_b(bn)
                max_part(b, 0, 2)
                if not last:
                    norm_c(bn)
                max_part(b, 0, 3)
                max_pair(b, 0)
                max_all(b, 0)
                sub(b, 0, 0)
                sub(b, 0, 1)
                if not last:
                    x_low(bn, 0)
                    x_low(bn, 1)
                sub(b, 0, 2)
                sub(b, 0, 3)
                if not last:
                    x_low(bn, 2)
                    x_low(bn, 3)
                split(b, 0, 0)
                split(b, 0, 1)
                for k in range(1, NK):
                    max_part(b, 1, k)
                max_pair(b, 1)
                max_all(b, 1)
                for step in ("T0", "T1", "P02", "T2", "P03", "T3", "B0", "B1", "T4", "T5", "B2", "B3", "T6", "T7"):
                    n = int(step[-1])
                    if step[0] == "T":
                        if not last:
                            t_low(bn, n)
                    elif step[0] == "P":
                        split(b, 0, n)
                    else:
                        sub(b, 1, n)
                inverse(b, 0)
                split(b, 1, 0)
                split(b, 1, 1)
                out_group(b, 0, bk["o", 0])
                split(b, 1, 2)
                out_group(b, 1, bk["o", 1])
                split(b, 1, 3)
                inverse(b, 1)
                for i in range(2, PER["o"]):
                    out_group(b, i, bk["o", i])
                if not last:
                    g_columns(bn)
                    for i in range(PER["u"]):
                        u_low(bn, i, bk["u", i])

            batches(dve, one)

        @block.tensor
        def _(pe):
            mm = nc.tensor.matmul

            def three(dst, parts, n):
                for k in range(n):
                    (wh, wl), (mh, ml) = parts(k)
                    mm(dst, wh, mh, start=(k == 0), stop=False)
                    mm(dst, wh, ml, start=False, stop=False)
                    ins = mm(dst, wl, mh, start=False, stop=(k == n - 1))
                return ins

            def t_group(bn, i, dst):
                ct, mh = i // NH, i % NH
                p = parity(bn)
                if i == 0:
                    wait(pe, xl_done, CT, bn, CT)
                w, m = slice(ct * P, ct * P + P), slice(mh * H, mh * H + H)
                three(dst[:, :], lambda k: ((ah[:, k, w], al[:, k, w]), (xh[p][:, k, m], xl[p][:, k, m])),
                      CT).then_inc(full["t"], 1)

            def u_group(bn, i, dst):
                p = parity(bn)
                w = slice(i * P, i * P + P)
                three(dst[:, :], lambda k: ((xh[p][:, k, w], xl[p][:, k, w]), (bh[:, k, :], bl[:, k, :])),
                      CT).then_inc(full["u"], 1)

            def s_group(b, i, dst):
                h, mt = i // MT, i % MT
                p = parity(b)
                if i == 0:
                    wait(pe, tl_done, PER["t"], b, PER["t"])
                w, n = slice(mt * P, mt * P + P), slice(h * H, h * H + H)
                three(dst[:, :], lambda k: ((th[:, k, w], tl[:, k, w]), (xh[p][:, k, n], xl[p][:, k, n])),
                      CT).then_inc(full["s"], 1)

            def o_group(b, i, dst):
                h, c = i // CT, i % CT
                w = slice(c * P, c * P + P)
                if i == 0:
                    wait(pe, evac["u"], PER["u"], b, PER["u"])
                for mt in range(MT):
                    hi, lo = chunk(h, mt // KC)
                    n = slice((mt % KC) * H, (mt % KC) * H + H)
                    if c == 0 and mt % KC == 0:
                        wait(pe, pl_done, NH * NK, b, NK * h + mt // KC + 1)
                    mm(dst[:, :], uh[:, mt, w], hi[:, n], start=(mt == 0), stop=False)
                    mm(dst[:, :], uh[:, mt, w], lo[:, n], start=False, stop=False)
                    ins = mm(dst[:, :], ul[:, mt, w], hi[:, n], start=False, stop=(mt == MT - 1))
                ins.then_inc(full["o"], 1)

            def group_means(bn):
                wait(pe, stat_step, STATS, bn, 2)
                mm(ps_small[:, 0:CT], gmean[:, :], mv[:, :, 0], start=True, stop=True).then_inc(stat_pe, 1)

            def group_vars(bn):
                wait(pe, stat_step, STATS, bn, 6)
                mm(ps_small[:, CT:2 * CT], gmean[:, :], dev[:, :], start=True, stop=True).then_inc(stat_pe, 1)

            b0 = (None, 0)
            pe.wait_ge(consts, 4)
            pe.wait_ge(wqk_in, 32)
            wq, wk, wv = w_qkv
            for t in range(CT):
                for o in range(CT):
                    ins = mm(bank[t][:, :], wk[:, o, t * P:t * P + P], wq[:, o, :], start=(o == 0), stop=(o == CT - 1))
                ins.then_inc(set_full, 1)
            pe.wait_ge(vec_ready, 3)
            for j in range(2 * CT):
                mm(ps_va[:, j:j + 1], vec[:, j // CT, (j % CT) * P:(j % CT + 1) * P], ones[:, 0:1], start=True, stop=True)
            mm(ps_va[:, 2 * CT:2 * CT + 1], ones[:, :], prod1[:, :], start=True, stop=True).then_inc(vec_full, 1)
            pe.wait_ge(wp_in, 16)
            for t in range(CT):
                g = CT + t
                if g >= MB:
                    pe.wait_ge(at_read, g - MB + 1)
                for o in range(CT):
                    ins = nc.tensor.transpose(bank[g % MB][:, o * P:o * P + P], w_p[:, o, t * P:t * P + P], ident[:, :])
                ins.then_inc(set_full, 1)
            pe.wait_ge(wv_in, 16)
            pe.wait_ge(wpt_read, CT)
            pe.wait_ge(at_read, CT)
            for t in range(CT):
                for o in range(CT):
                    ins = mm(bank[(2 * CT + t) % MB][:, :], wv[:, o, t * P:t * P + P], w_pt[:, o, :],
                             start=(o == 0), stop=(o == CT - 1))
                ins.then_inc(set_full, 1)
                if t == 1:
                    group_means(b0)
                if t == 2:
                    group_vars(b0)

            pe.wait_ge(a_split, 1)
            pe.wait_ge(bt_read, CT)
            for g, (kind, i) in enumerate(PROLOGUE):
                if g >= MB:
                    k, j = PROLOGUE[g - MB]
                    pe.wait_ge(evac[k], j + 1)
                if (kind, i) == ("u", 0):
                    pe.wait_ge(vo_ready, 1)
                    for t in range(CT):
                        ins = mm(ps_vb[:, t:t + 1], vec_o[:, t * P:t * P + P], ones[:, 0:1], start=True, stop=True)
                    ins.then_inc(vo_full, 1)
                    pe.wait_ge(scratch_free, 1)
                (t_group if kind == "t" else u_group)(b0, i, bank[g % MB])

            def one(b, last):
                bn = nxt(b)
                seq = LAST if last else BATCH
                for n, (kind, i) in enumerate(seq):
                    if n >= MB:
                        k, j = seq[n - MB]
                        if k in "so":
                            wait(pe, evac[k], PER[k], b, j + 1)
                        else:
                            wait(pe, evac[k], PER[k], bn, j + 1)
                    else:
                        k, j = BATCH[n - MB]
                        wait(pe, evac[k], PER[k], b, j + 1)
                    dst = bank[(BASE + n) % MB]
                    if kind == "s":
                        s_group(b, i, dst)
                        if i == 4 and not last:
                            group_means(bn)
                        if i == 6 and not last:
                            group_vars(bn)
                    elif kind == "t":
                        t_group(bn, i, dst)
                    elif kind == "o":
                        o_group(b, i, dst)
                    else:
                        u_group(bn, i, dst)

            batches(pe, one)


_INS = ["x", "L0_conv_gamma", "L0_conv_beta", "L0_conv_qkv_w", "L0_conv_qkv_b", "L0_conv_proj_w", "L0_conv_proj_b"]


def kernel(**inputs):
    import numpy as _np
    import concourse.bacc as _bacc
    from concourse import mybir as _mybir
    from concourse.bass_utils import run_bass_kernel_spmd as _run

    nc = _bacc.Bacc("TRN2", target_bir_lowering=False, num_devices=1)
    arrays, args = {}, []
    for name in _INS:
        a = _np.ascontiguousarray(inputs[name])
        arrays[f"in_{name}"] = a
        args.append(nc.dram_tensor(f"in_{name}", a.shape, _mybir.dt.from_np(a.dtype), kind="ExternalInput").ap())
    shape = arrays["in_x"].shape
    args.append(nc.dram_tensor("out_0", shape, _mybir.dt.float32, kind="ExternalOutput").ap())
    attention_block_kernel(nc, *args)
    r = _run(nc, [arrays], core_ids=[0])
    return r.results[0]["out_0"]
```

```python
import math
from contextlib import ExitStack

import concourse.bass as bass
from concourse import mybir


def attention_block_kernel(nc, x, gamma, beta, qkv_w, qkv_b, proj_w, proj_b, out):
    fp32, fp16, i32 = mybir.dt.float32, mybir.dt.float16, mybir.dt.int32
    ALU, ACT, AX = mybir.AluOpType, mybir.ActivationFunctionType, mybir.AxisListType

    P = 128
    NB, C, HH, WW = x.shape
    N = HH * WW
    GROUP = C // 32
    EPS = 1e-5
    CT, MT = C // P, N // P
    H = 512
    NH = N // H
    KC = 2
    NK = MT // KC
    Q = 32
    SCALE = 1.0 / math.sqrt(C)
    XMAX = 128.0
    W_TOP = 2.0 ** 14
    T_TOP = 2.0 ** 15
    MAXES = 9
    SUMS = 10
    NEWTON = 3
    STATS = 9 + 3 * NEWTON
    U_SCALE = T_TOP / (C * XMAX * W_TOP)
    P_LOG = 11 * math.log(2.0)

    MB = 5
    VO_AT = 2
    BATCH = ([("s", i) for i in range(NH * MT)] + [("t", i) for i in range(CT * NH)]
             + [("o", i) for i in range(NH * CT)] + [("u", i) for i in range(MT)])
    LAST = [g for g in BATCH if g[0] in "so"]
    PROLOGUE = [g for g in BATCH if g[0] in "tu"]
    PER = {"s": NH * MT, "t": CT * NH, "o": NH * CT, "u": MT}
    assert len(BATCH) % MB == 0
    BASE = len(PROLOGUE) % MB

    x_d = x.rearrange("b (t p) h w -> b p t (h w)", p=P)
    w_parts = qkv_w.rearrange("(s t p) c -> s p t c", s=3, p=P)
    out_d = out.rearrange("b (t p) h w -> b p t (h w)", p=P)

    ctx = ExitStack()
    with ctx:
        def sb(name, shape, dt=fp32):
            return ctx.enter_context(nc.sbuf_tensor(name, shape, dt))

        def pb(name):
            return ctx.enter_context(nc.psum_tensor(name, [P, 512], fp32))

        def sem(name):
            return ctx.enter_context(nc.semaphore(name))

        xs = [sb(f"x{p}", [P, CT, N]) for p in range(2)]
        xh = [sb(f"xh{p}", [P, CT, N], fp16) for p in range(2)]
        xl = [sb(f"xl{p}", [P, CT, N], fp16) for p in range(2)]
        xf = sb("xf", [P, 2, N])
        th = sb("th", [P, CT, N], fp16)
        tl = sb("tl", [P, CT, N], fp16)
        tf = sb("tf", [P, 4, H])
        uh = sb("uh", [P, MT, C], fp16)
        ul = sb("ul", [P, MT, C], fp16)
        sp = [sb(f"sp{h}", [P, MT, H]) for h in range(NH)]
        pf = sb("pf", [P, 2, KC, H])
        ah = sb("ah", [P, CT, C], fp16)
        al = sb("al", [P, CT, C], fp16)
        bh = sb("bh", [P, CT, C], fp16)
        bl = sb("bl", [P, CT, C], fp16)
        ob = sb("ob", [P, CT, H])
        mx = sb("mx", [P, 2, H])
        tr = sb("tr", [P, H])
        maxb = sb("maxb", [P, H])
        ps2 = sb("ps2", [P, KC, H])
        rinv = [sb(f"rinv{h}", [P, H]) for h in range(NH)]
        gacc = sb("gacc", [P, N])
        gcol = sb("gcol", [P, MT])
        gq = sb("gq", [P, N // Q])
        gg = sb("gg", [P, P // Q, MT])
        gs = sb("gs", [P, MT])
        gr = sb("gr", [P, CT])
        gn = sb("gn", [P, CT])
        g0 = sb("g0", [P, 1])
        st = sb("st", [P, CT, 2, 6])
        mv = sb("mv", [P, CT, 2])
        dev = sb("dev", [P, CT])
        var = sb("var", [P, CT])
        rs = sb("rs", [P, CT])
        nt = sb("nt", [P, CT])
        mg = sb("mg", [P, CT])
        nb = sb("nb", [P, CT])
        rq = sb("rq", [P, H // Q])
        rg = sb("rg", [Q, P // Q, H // Q])
        r1 = sb("r1", [Q, H // Q])
        mb = sb("mb", [P, H // Q])
        ident = sb("ident", [P, P])
        gmean = sb("gmean", [P, P])
        ones = sb("ones", [P, P])
        ebias = sb("ebias", [P, 1])
        gam = sb("gam", [P, CT])
        qkvb = sb("qkvb", [P, 3 * CT])
        projb = sb("projb", [P, CT])
        bdot = sb("bdot", [P, 3 * CT])
        bt = sb("bt", [P, 3 * CT])
        prod = sb("prod", [P, CT])
        prod1 = sb("prod1", [P, 1])
        am = sb("am", [P, 2])
        amr = sb("amr", [P, 2])
        bm = sb("bm", [P, 1])
        bmr = sb("bmr", [P, 1])
        s0 = sb("s0", [P, 3])
        s1 = sb("s1", [P, 3])
        sc = sb("sc", [P, 3])
        si = sb("si", [P, 3])
        ft = sb("ft", [P, 1])
        esc = sb("esc", [P, 1])
        cu = sb("cu", [P, 1])
        ta = sb("ta", [P, CT])
        gw = sb("gw", [P, CT])
        gc = sb("gc", [P, 1])
        obias = sb("obias", [P, CT])
        w_qkv = [sp[0][:, 0:CT, :], sp[0][:, CT:2 * CT, :], sp[1][:, 0:CT, :]]
        w_p = sp[1][:, CT:2 * CT, :]
        w_pt = pf[:, :, :, :].rearrange("p a b n -> p (a b) n")
        at32 = xs[1][:, 0:2, :].rearrange("p a (b n) -> p (a b) n", n=C)
        bt32 = xs[1][:, 2:4, :].rearrange("p a (b n) -> p (a b) n", n=C)
        gam_row, beta_row, junk = maxb[:, :], rinv[0][:, :], rinv[1][:, :]
        vec = gacc[:, :].rearrange("p (a n) -> p a n", a=2)
        vec_o = ps2[:, 0, :]

        bank = [pb(f"bank{i}") for i in range(MB)]
        ps_small, ps_va, ps_vb = pb("ps_small"), pb("ps_va"), pb("ps_vb")

        beta_in, gamma_in, projb_in = sem("beta_in"), sem("gamma_in"), sem("projb_in")
        wqk_in, wp_in, wv_in = [sem(f"wqk{o}_in") for o in range(CT)], sem("wp_in"), sem("wv_in")
        x0_in = [sem(f"x0_in{c}") for c in range(CT)]
        x_in = [sem("x_in0"), sem("x_in1")]
        masks, consts = sem("masks"), sem("consts")
        set_full, set_step, scratch_free = sem("set_full"), sem("set_step"), sem("scratch_free")
        at_read, wpt_read, bt_read = sem("at_read"), sem("wpt_read"), sem("bt_read")
        vec_ready, vec_full, vo_ready, vo_full = sem("vec_ready"), sem("vec_full"), sem("vo_ready"), sem("vo_full")
        am_ready, absmax, bm_ready, bsmax = sem("am_ready"), sem("absmax"), sem("bm_ready"), sem("bsmax")
        ta_ready, a_scale, b_scale, ah_done, bh_done, a_split = (
            sem("ta_ready"), sem("a_scale"), sem("b_scale"), sem("ah_done"), sem("bh_done"), sem("a_split"))
        full = {k: sem(f"{k}_full") for k in "stou"}
        evac = {k: sem(f"{k}_evac") for k in "stou"}
        stat_step, stat_pe = sem("stat_step"), sem("stat_pe")
        rs_ready, xf_done, xh_done, xl_done = sem("rs_ready"), sem("xf_done"), sem("xh_done"), sem("xl_done")
        g_step, g_ready = sem("g_step"), sem("g_ready")
        tf_done, tl_done, uh_done = sem("tf_done"), sem("tl_done"), sem("uh_done")
        max_step, max_ready, sub_done = sem("max_step"), sem("max_ready"), sem("sub_done")
        pf_done, ph_done, pl_done = sem("pf_done"), sem("ph_done"), sem("pl_done")
        sum_step, rinv_done = sem("sum_step"), sem("rinv_done")
        out_ready, stored, stored_last = sem("out_ready"), sem("stored"), sem("stored_last")

        def count(per, batch, off):
            reg, c = batch
            return per * c + off if reg is None else reg * per + (per * c + off)

        def wait(eng, s, per, batch, off):
            reg, c = batch
            if reg is None:
                if per * c + off > 0:
                    eng.wait_ge(s, per * c + off)
            else:
                assert per * (c + 1) + off > 0
                eng.wait_ge(s, count(per, batch, off))

        def parity(batch):
            reg, c = batch
            return c % 2 if reg is None else (c + 1) % 2

        def nxt(batch):
            return batch[0], batch[1] + 1

        def chunk(h, k):
            v = sp[h][:, KC * k:KC * k + KC, :].bitcast(fp16).rearrange("p a n -> p (a n)")
            return v[:, 0:KC * H], v[:, KC * H:2 * KC * H]

        def last_half(b, h):
            return b[0] is None and b[1] == NB - 1 and h == NH - 1

        def spare(b, h, k):
            return last_half(b, h) and k >= 2

        def slot(b, h, k):
            place = tf[:, :, :].rearrange("p (a b) n -> p a b n", b=KC) if spare(b, h, k) else pf[:, :, :, :]
            return place[:, k % 2, :, :]

        def outs(b, h):
            if last_half(b, h):
                return xf[:, :, :].rearrange("p a (b n) -> p (a b) n", n=H)
            return ob[:, :, :]

        def batches(eng, one):
            one((None, 0), False)
            with eng.Fori(1, NB - 2, 2) as r:
                one((r, 0), False)
                one((r, 1), False)
            one((None, NB - 1), True)

        block = ctx.enter_context(nc.Block())

        @block.sync
        def _(sp_eng):
            with nc.allow_non_contiguous_dma(reason="gamma, a value per partition"):
                sp_eng.dma_start(gam[:, :], gamma.rearrange("(t p) -> p t", p=P)).then_inc(gamma_in, 16)
            for o in range(CT):
                sp_eng.dma_start(w_qkv[0][:, o, :], w_parts[0][:, o, :]).then_inc(wqk_in[o], 16)
                sp_eng.dma_start(w_qkv[1][:, o, :], w_parts[1][:, o, :]).then_inc(wqk_in[o], 16)
            sp_eng.dma_start(w_p, proj_w.rearrange("(t p) c -> p t c", p=P)).then_inc(wp_in, 16)
            sp_eng.dma_start(w_qkv[2], w_parts[2]).then_inc(wv_in, 16)
            for c in range(CT):
                sp_eng.dma_start(xs[0][:, c, :], x_d[0][:, c, :]).then_inc(x0_in[c], 16)

            def one(b, last):
                if not last:
                    nxt_b = nxt(b)
                    if b[0] is None and b[1] == 0:
                        sp_eng.wait_ge(scratch_free, 1)
                    wait(sp_eng, out_ready, PER["o"], b, 0)
                    src = x_d[1] if b[0] is None else x_d[b[0] + nxt_b[1]]
                    sp_eng.dma_start(xs[parity(nxt_b)][:, :, :], src).then_inc(x_in[parity(nxt_b)], 16)
                for h in range(NH):
                    dst = out_d[b[1]] if b[0] is None else out_d[b[0] + b[1]]
                    if last and h == NH - 1:
                        for c in range(CT):
                            wait(sp_eng, out_ready, PER["o"], b, CT * h + c + 1)
                            sp_eng.dma_start(dst[:, c, h * H:(h + 1) * H], outs(b, h)[:, c, :]).then_inc(stored_last, 16)
                    else:
                        wait(sp_eng, out_ready, PER["o"], b, CT * (h + 1))
                        sp_eng.dma_start(dst[:, :, h * H:(h + 1) * H], ob[:, :, :]).then_inc(stored, 16)

            batches(sp_eng, one)
            sp_eng.wait_ge(stored, 16 * (NH * NB - 1))
            sp_eng.wait_ge(stored_last, 16 * CT)

        @block.gpsimd
        def _(pool):
            nc.gpsimd.memset(ident[:, :], 0.0).then_inc(masks, 1)
            nc.gpsimd.memset(gmean[:, :], 1.0 / GROUP).then_inc(masks, 1)
            nc.gpsimd.memset(ones[:, :], 1.0).then_inc(consts, 1)
            nc.gpsimd.memset(ebias[:, :], P_LOG).then_inc(consts, 1)
            pool.wait_ge(masks, 2)
            nc.gpsimd.affine_select(out=ident[:, :], in_=ident[:, :], compare_op=ALU.not_equal, fill=1.0,
                                    base=0, pattern=[[-1, P]], channel_multiplier=1).then_inc(consts, 1)
            blocks = gmean[:, :].rearrange("p (g j) -> p g j", j=GROUP)
            nc.gpsimd.affine_select(out=blocks, in_=blocks, compare_op=ALU.is_ge, fill=0.0, base=0,
                                    pattern=[[-GROUP, P // GROUP], [0, GROUP]], channel_multiplier=1).then_inc(masks, 1)
            pool.wait_ge(masks, 3)
            nc.gpsimd.affine_select(out=blocks, in_=blocks, compare_op=ALU.is_ge, fill=0.0, base=GROUP - 1,
                                    pattern=[[GROUP, P // GROUP], [0, GROUP]], channel_multiplier=-1).then_inc(consts, 1)
            pool.wait_ge(am_ready, 1)
            nc.gpsimd.partition_all_reduce(amr[:, :], am[:, :], P, bass.bass_isa.ReduceOp.absmax).then_inc(absmax, 1)
            pool.wait_ge(bm_ready, 1)
            nc.gpsimd.partition_all_reduce(bmr[:, :], bm[:, :], P, bass.bass_isa.ReduceOp.absmax).then_inc(bsmax, 1)

        @block.scalar
        def _(act):
            act.dma_start(beta_row, beta.partition_broadcast(P)).then_inc(beta_in, 16)
            with nc.allow_non_contiguous_dma(reason="biases, a value per partition"):
                act.dma_start(qkvb[:, :], qkv_b.rearrange("(t p) -> p t", p=P)).then_inc(beta_in, 16)
                act.dma_start(gam_row, gamma.partition_broadcast(P)).then_inc(gamma_in, 16)
                act.dma_start(projb[:, :], proj_b.rearrange("(t p) -> p t", p=P)).then_inc(projb_in, 16)

            def x_norm(bn, c):
                p = parity(bn)
                wait(act, rs_ready, 1, bn, 1)
                wait(act, xl_done, CT, bn, c - 1)
                nc.scalar.activation(xf[:, c % 2, :], xs[p][:, c, :], ACT.Identity,
                                     bias=nb[:, c:c + 1], scale=rs[:, c:c + 1]).then_inc(xf_done, 1)
                nc.scalar.activation(xh[p][:, c, :], xs[p][:, c, :], ACT.Identity,
                                     bias=nb[:, c:c + 1], scale=rs[:, c:c + 1]).then_inc(xh_done, 1)

            def t_group(bn, i, bk):
                ct, mh = i // NH, i % NH
                wait(act, full["t"], PER["t"], bn, i + 1)
                wait(act, tl_done, PER["t"], bn, i - 3)
                nc.scalar.activation(tf[:, i % 4, :], bk[:, :], ACT.Identity,
                                     bias=ta[:, ct:ct + 1], scale=ft[:, 0:1]).then_inc(tf_done, 1)
                nc.scalar.activation(th[:, ct, mh * H:(mh + 1) * H], bk[:, :], ACT.Identity,
                                     bias=ta[:, ct:ct + 1], scale=ft[:, 0:1]).then_inc(evac["t"], 1)

            def u_group(bn, i, bk):
                wait(act, full["u"], PER["u"], bn, i + 1)
                nc.scalar.activation(uh[:, i, :], bk[:, :], ACT.Copy, scale=U_SCALE).then_inc(uh_done, 1)

            def s_group(b, i, bk):
                h, mt = i // MT, i % MT
                wait(act, full["s"], PER["s"], b, i + 1)
                if i == 0:
                    wait(act, g_ready, 1, b, 1)
                if mt == 0:
                    wait(act, full["o"], PER["o"], b, CT * (h + 1) - PER["o"])
                nc.scalar.activation(sp[h][:, mt, :], bk[:, :], ACT.Identity,
                                     bias=gcol[:, mt:mt + 1]).then_inc(evac["s"], 1)

            def exps(b, h, k):
                n = NK * h + k
                wait(act, sub_done, NH * NK, b, n + 1)
                if not spare(b, h, k):
                    wait(act, sum_step, NH * SUMS, b, SUMS * h + (1 if k >= 2 else k + 2 - SUMS))
                nc.scalar.activation(slot(b, h, k), sp[h][:, KC * k:KC * k + KC, :], ACT.Exp,
                                     bias=ebias[:, 0:1], scale=esc[:, 0:1]).then_inc(pf_done, 1)

            def high(b, h, k):
                wait(act, pf_done, NH * NK, b, NK * h + k + 1)
                hi, _ = chunk(h, k)
                nc.scalar.activation(hi, slot(b, h, k).rearrange("p a n -> p (a n)"), ACT.Copy).then_inc(ph_done, 1)

            b0 = (None, 0)
            act.wait_ge(consts, 4)
            act.wait_ge(gamma_in, 32)
            for t in range(CT):
                act.wait_ge(set_full, CT + t + 1)
                nc.scalar.activation(w_pt[:, t, :], bank[(CT + t) % MB][:, :], ACT.Copy).then_inc(wpt_read, 1)
            act.wait_ge(a_scale, 1)
            nc.scalar.activation(ah[:, :, :], at32, ACT.Copy, scale=sc[:, 0:1]).then_inc(ah_done, 1)
            for t in range(CT):
                act.wait_ge(set_full, 2 * CT + t + 1)
                nc.scalar.activation(bt32[:, t, :], bank[(2 * CT + t) % MB][:, :], ACT.Copy,
                                     scale=gam[:, t:t + 1]).then_inc(bt_read, 1)
            act.wait_ge(rs_ready, 1)
            for c in range(CT):
                nc.scalar.activation(xh[0][:, c, :], xs[0][:, c, :], ACT.Identity,
                                     bias=nb[:, c:c + 1], scale=rs[:, c:c + 1]).then_inc(xh_done, 1)
            act.wait_ge(ta_ready, 1)
            for i in range(CT):
                t_group(b0, i, bank[i % MB])
            act.wait_ge(b_scale, 1)
            nc.scalar.activation(bh[:, :, :], bt32, ACT.Copy, scale=sc[:, 2:3]).then_inc(bh_done, 1)
            for i in range(CT, PER["t"]):
                t_group(b0, i, bank[i % MB])
            for i in range(PER["u"]):
                u_group(b0, i, bank[(PER["t"] + i) % MB])

            def one(b, last):
                bn = nxt(b)
                seq = LAST if last else BATCH
                bk = {g: bank[(BASE + n) % MB] for n, g in enumerate(seq)}
                for i in range(MT):
                    s_group(b, i, bk["s", i])
                s1_order = ["S0", "S1", "E0", "E1", "S2", "H0", "H1", "S3", "E2", "S4", "E3", "H2", "H3", "S5", "S6",
                            "S7"] if last else ["X0", "S0", "X1", "S1", "E0", "S2", "E1", "X2", "S3", "S4", "X3", "S5", "S6", "S7"]
                for step in s1_order:
                    n = int(step[1])
                    if step[0] == "S":
                        s_group(b, MT + n, bk["s", MT + n])
                    elif step[0] == "X":
                        x_norm(bn, n)
                    else:
                        (exps if step[0] == "E" else high)(b, 0, n)
                t_order = ["E10", "E11", "H10", "H11", "E12", "H12", "E13", "H13"] if last else ["H00", "H01", "T0", "E02", "T1", "E03", "H02", "T2", "H03", "T3", "T4",
                           "E10", "T5", "E11", "T6", "H10", "T7", "H11", "E12", "H12", "E13", "H13"]
                for step in t_order:
                    if step[0] == "T":
                        t_group(bn, int(step[1]), bk["t", int(step[1])])
                    else:
                        (exps if step[0] == "E" else high)(b, int(step[1]), int(step[2]))
                if not last:
                    for i in range(MT):
                        u_group(bn, i, bk["u", i])

            batches(act, one)

        @block.vector
        def _(dve):
            v = nc.vector
            steps = [0]

            def link(ins):
                steps[0] += 1
                ins.then_inc(set_step, 1)
                dve.wait_ge(set_step, steps[0])

            def stats(bn, i):
                p = parity(bn)
                if bn[0] is None and bn[1] == 0:
                    if i % 2 == 0:
                        dve.wait_ge(x0_in[i // 2], 16)
                elif i == 0:
                    wait(dve, x_in[p], 8, bn, 8 * p)
                ins = v.bn_stats(st[:, i // 2, i % 2, :], xs[p][:, i // 2, (i % 2) * 512:(i % 2 + 1) * 512])
                if i == 2 * CT - 1:
                    ins.then_inc(stat_step, 1)

            def norm_a(bn):
                for c in range(CT):
                    ins = v.bn_aggr(mv[:, c, :], st[:, c, :, :].rearrange("p a b -> p (a b)"))
                ins.then_inc(stat_step, 1)

            def norm_b(bn):
                wait(dve, stat_pe, 2, bn, 1)
                v.tensor_copy(mg[:, :], ps_small[:, 0:CT]).then_inc(stat_step, 1)
                wait(dve, stat_step, STATS, bn, 3)
                v.tensor_tensor(dev[:, :], mv[:, :, 0], mg[:, :], ALU.subtract).then_inc(stat_step, 1)
                wait(dve, stat_step, STATS, bn, 4)
                v.tensor_tensor(var[:, :], dev[:, :], dev[:, :], ALU.mult).then_inc(stat_step, 1)
                wait(dve, stat_step, STATS, bn, 5)
                v.tensor_tensor(dev[:, :], var[:, :], mv[:, :, 1], ALU.add).then_inc(stat_step, 1)

            def norm_c(bn):
                wait(dve, stat_pe, 2, bn, 2)
                v.tensor_scalar(var[:, :], ps_small[:, CT:2 * CT], EPS, None, ALU.add).then_inc(stat_step, 1)
                wait(dve, stat_step, STATS, bn, 7)
                v.tensor_single_scalar(nt[:, :].bitcast(i32), var[:, :].bitcast(i32), 1,
                                       ALU.logical_shift_right).then_inc(stat_step, 1)
                wait(dve, stat_step, STATS, bn, 8)
                v.tensor_scalar(rs[:, :].bitcast(i32), nt[:, :].bitcast(i32), -1.0, float(0x5F3759DF),
                                ALU.mult, ALU.add).then_inc(stat_step, 1)
                for k in range(NEWTON):
                    wait(dve, stat_step, STATS, bn, 9 + 3 * k)
                    v.tensor_tensor(nt[:, :], rs[:, :], rs[:, :], ALU.mult).then_inc(stat_step, 1)
                    wait(dve, stat_step, STATS, bn, 10 + 3 * k)
                    v.scalar_tensor_tensor(out=dev[:, :], in0=nt[:, :], scalar=-0.5, in1=var[:, :],
                                           op0=ALU.mult, op1=ALU.mult).then_inc(stat_step, 1)
                    wait(dve, stat_step, STATS, bn, 11 + 3 * k)
                    v.scalar_tensor_tensor(out=rs[:, :], in0=dev[:, :], scalar=1.5, in1=rs[:, :],
                                           op0=ALU.add, op1=ALU.mult).then_inc(stat_step, 1)
                wait(dve, stat_step, STATS, bn, STATS)
                v.scalar_tensor_tensor(out=nb[:, :], in0=mg[:, :], scalar=-1.0, in1=rs[:, :],
                                       op0=ALU.mult, op1=ALU.mult).then_inc(rs_ready, 1)

            def x_low(bn, c):
                p = parity(bn)
                wait(dve, xf_done, CT, bn, c + 1)
                wait(dve, xh_done, CT, bn, c + 1)
                v.tensor_tensor(xl[p][:, c, :], xf[:, c % 2, :], xh[p][:, c, :], ALU.subtract).then_inc(xl_done, 1)

            G = 11

            def g_columns(bn):
                x_b = xs[parity(bn)]
                v.tensor_tensor(gr[:, :], gw[:, :], rs[:, :], ALU.mult).then_inc(g_step, 1)
                v.tensor_tensor(gn[:, :], gw[:, :], nb[:, :], ALU.mult).then_inc(g_step, 1)
                wait(dve, g_step, G, bn, 2)
                v.tensor_reduce(g0[:, :], gn[:, :], axis=AX.X, op=ALU.add).then_inc(g_step, 1)
                wait(dve, g_step, G, bn, 3)
                v.tensor_scalar(gacc[:, :], x_b[:, 0, :], gr[:, 0:1], g0[:, 0:1], ALU.mult, ALU.add).then_inc(g_step, 1)
                for c in range(1, CT):
                    wait(dve, g_step, G, bn, 3 + c)
                    v.scalar_tensor_tensor(out=gacc[:, :], in0=x_b[:, c, :], scalar=gr[:, c:c + 1],
                                           in1=gacc[:, :], op0=ALU.mult, op1=ALU.add).then_inc(g_step, 1)
                flat = mx[:, :, :].rearrange("p a n -> p (a n)")
                wait(dve, g_step, G, bn, 7)
                v.transpose(flat, gacc[:, :]).then_inc(g_step, 1)
                wait(dve, g_step, G, bn, 8)
                v.tensor_reduce(gq[:, :], flat.rearrange("p (k i) -> p k i", i=Q), axis=AX.X,
                                op=ALU.add).then_inc(g_step, 1)
                wait(dve, g_step, G, bn, 9)
                for a in range(P // Q):
                    for q in range(P // Q):
                        ins = v.tensor_copy(gg[Q * a:Q * a + Q, q, :], gq[Q * q:Q * q + Q, a:N // Q:P // Q])
                ins.then_inc(g_step, 1)
                wait(dve, g_step, G, bn, 10)
                v.tensor_reduce(gs[:, :], gg[:, :, :].rearrange("p q m -> p m q"), axis=AX.X,
                                op=ALU.add).then_inc(g_step, 1)
                wait(dve, g_step, G, bn, 11)
                v.tensor_scalar(gcol[:, :], gs[:, :], gc[:, 0:1], None, ALU.add).then_inc(g_ready, 1)

            def t_low(bn, i):
                ct, mh = i // NH, i % NH
                wait(dve, tf_done, PER["t"], bn, i + 1)
                wait(dve, evac["t"], PER["t"], bn, i + 1)
                v.tensor_tensor(tl[:, ct, mh * H:(mh + 1) * H], tf[:, i % 4, :], th[:, ct, mh * H:(mh + 1) * H],
                                ALU.subtract).then_inc(tl_done, 1)

            def u_low(bn, i, bk):
                wait(dve, uh_done, PER["u"], bn, i + 1)
                v.scalar_tensor_tensor(out=ul[:, i, :], in0=bk[:, :], scalar=U_SCALE, in1=uh[:, i, :],
                                       op0=ALU.mult, op1=ALU.subtract).then_inc(evac["u"], 1)

            def max_part(b, h, k):
                if k == 0:
                    return
                a, c = NH * MAXES, MAXES * h
                wait(dve, evac["s"], PER["s"], b, MT * h + KC * (k + 1))
                if k >= 2:
                    wait(dve, max_step, a, b, c + k - 1)
                first = sp[h][:, 0:KC, :] if k == 1 else mx[:, :, :]
                v.tensor_tensor(mx[:, :, :], first, sp[h][:, KC * k:KC * k + KC, :], ALU.max).then_inc(max_step, 1)

            def max_pair(b, h):
                wait(dve, max_step, NH * MAXES, b, MAXES * h + 3)
                v.tensor_tensor(mx[:, 0, :], mx[:, 0, :], mx[:, 1, :], ALU.max).then_inc(max_step, 1)

            def across(src, dst, op, b, step, per, c, done, invert=False):
                wait(dve, step, per, b, c)
                v.transpose(tr[:, :], src).then_inc(step, 1)
                wait(dve, step, per, b, c + 1)
                v.tensor_reduce(rq[:, :], tr[:, :].rearrange("p (k i) -> p k i", i=Q), axis=AX.X, op=op).then_inc(step, 1)
                wait(dve, step, per, b, c + 2)
                for q in range(P // Q):
                    ins = v.tensor_copy(rg[:, q, :], rq[Q * q:Q * q + Q, :])
                ins.then_inc(step, 1)
                wait(dve, step, per, b, c + 3)
                v.tensor_reduce(r1[:, :], rg[:, :, :].rearrange("p q k -> p k q"), axis=AX.X, op=op).then_inc(step, 1)
                wait(dve, step, per, b, c + 4)
                if invert:
                    v.reciprocal(r1[:, :], r1[:, :]).then_inc(step, 1)
                    c += 1
                    wait(dve, step, per, b, c + 4)
                for q in range(P // Q):
                    ins = v.tensor_copy(mb[Q * q:Q * q + Q, :], r1[:, :])
                ins.then_inc(step, 1)
                wait(dve, step, per, b, c + 5)
                v.transpose(dst.rearrange("p (k i) -> p k i", i=Q),
                            mb[:, :].unsqueeze(2).to_broadcast([P, H // Q, Q])).then_inc(done, 1)

            def max_all(b, h):
                across(mx[:, 0, :], maxb[:, :], ALU.max, b, max_step, NH * MAXES, MAXES * h + 4, max_ready)

            def sub(b, h, k):
                if k == 0:
                    wait(dve, max_ready, NH, b, h + 1)
                tile = sp[h][:, KC * k:KC * k + KC, :]
                v.tensor_tensor(tile, tile, maxb[:, :].unsqueeze(1).to_broadcast([P, KC, H]),
                                ALU.subtract).then_inc(sub_done, 1)

            def split(b, h, k):
                a, c = NH * SUMS, SUMS * h
                wait(dve, ph_done, NH * NK, b, NK * h + k + 1)
                hi, lo = chunk(h, k)
                v.tensor_tensor(lo, slot(b, h, k).rearrange("p a n -> p (a n)"), hi, ALU.subtract).then_inc(pl_done, 1)
                if k == 1:
                    v.tensor_tensor(ps2[:, :, :], pf[:, 0, :, :], pf[:, 1, :, :], ALU.add).then_inc(sum_step, 1)
                elif k >= 2:
                    wait(dve, sum_step, a, b, c + k - 1)
                    v.tensor_tensor(ps2[:, :, :], ps2[:, :, :], slot(b, h, k), ALU.add).then_inc(sum_step, 1)

            def inverse(b, h):
                wait(dve, sum_step, NH * SUMS, b, SUMS * h + 3)
                v.tensor_tensor(ps2[:, 0, :], ps2[:, 0, :], ps2[:, 1, :], ALU.add).then_inc(sum_step, 1)
                across(ps2[:, 0, :], rinv[h][:, :], ALU.add, b, sum_step, NH * SUMS, SUMS * h + 4, rinv_done, invert=True)

            def out_group(b, i, bk):
                h, c = i // CT, i % CT
                wait(dve, full["o"], PER["o"], b, i + 1)
                if c == 0:
                    wait(dve, rinv_done, NH, b, h + 1)
                    if not last_half(b, h):
                        wait(dve, stored, 16 * NH, b, 16 * h)
                o = outs(b, h)[:, c, :]
                v.scalar_tensor_tensor(out=o, in0=bk[:, :], scalar=cu[:, 0:1], in1=rinv[h][:, :],
                                       op0=ALU.mult, op1=ALU.mult).then_inc(evac["o"], 1)
                wait(dve, evac["o"], PER["o"], b, i + 1)
                v.scalar_tensor_tensor(out=o, in0=o, scalar=obias[:, c:c + 1],
                                       in1=xs[parity(b)][:, c, h * H:(h + 1) * H],
                                       op0=ALU.add, op1=ALU.add).then_inc(out_ready, 1)

            b0 = (None, 0)

            def bias_dots(s):
                for t in range(CT):
                    if s == 1:
                        dve.wait_ge(wqk_in[t], 32)
                    j = CT * s + t
                    link(v.tensor_tensor_reduce(out=junk, in0=w_qkv[s][:, t, :], in1=beta_row, scale=1.0, scalar=0.0,
                                                op0=ALU.mult, op1=ALU.add, accum_out=bdot[:, j:j + 1]))
                r = slice(CT * s, CT * s + CT)
                link(v.tensor_tensor(bt[:, r], bdot[:, r], qkvb[:, r], ALU.add))

            def tile_sums(dst, w, s, done):
                link(v.tensor_scalar(dst, w[:, 0, :], bt[:, CT * s:CT * s + 1], None, ALU.mult))
                for o in range(1, CT):
                    ins = v.scalar_tensor_tensor(out=dst, in0=w[:, o, :], scalar=bt[:, CT * s + o:CT * s + o + 1],
                                                 in1=dst, op0=ALU.mult, op1=ALU.add)
                    if o < CT - 1:
                        link(ins)
                ins.then_inc(done, 1)

            def powers(dst, src, top):
                link(v.reciprocal(s1[:, dst], src))
                link(v.tensor_scalar(s0[:, dst], s1[:, dst], top, None, ALU.mult))
                link(v.tensor_single_scalar(sc[:, dst].bitcast(i32), s0[:, dst].bitcast(i32), 0x7F800000, ALU.bitwise_and))
                link(v.reciprocal(si[:, dst], sc[:, dst]))

            dve.wait_ge(beta_in, 32)
            bias_dots(1)
            tile_sums(vec[:, 0, :], w_qkv[0], 1, vec_ready)
            bias_dots(0)
            dve.wait_ge(gamma_in, 32)
            for t in range(CT):
                dve.wait_ge(set_full, t + 1)
                v.scalar_tensor_tensor(out=at32[:, t, :], in0=bank[t % MB][:, :], scalar=gam[:, t:t + 1],
                                       in1=gam_row, op0=ALU.mult, op1=ALU.mult).then_inc(at_read, 1)
            dve.wait_ge(at_read, CT)
            link(v.tensor_reduce(am[:, 0:1], at32, axis=AX.XY, op=ALU.max, apply_absolute_value=True))
            dve.wait_ge(vec_full, 1)
            link(v.tensor_tensor(ta[:, :], ps_va[:, 0:CT], gam[:, :], ALU.mult))
            v.tensor_reduce(am[:, 1:2], ta[:, :], axis=AX.X, op=ALU.max, apply_absolute_value=True).then_inc(am_ready, 1)
            for i in range(2):
                stats(b0, i)
            dve.wait_ge(absmax, 1)
            link(v.tensor_scalar(s0[:, 0:1], amr[:, 0:1], 1e-30, None, ALU.max))
            powers(slice(0, 1), s0[:, 0:1], W_TOP)
            link(v.tensor_scalar(s1[:, 2:3], amr[:, 0:1], 1e-30, None, ALU.max))
            link(v.scalar_tensor_tensor(out=s0[:, 1:2], in0=s1[:, 2:3], scalar=C * XMAX, in1=amr[:, 1:2],
                                        op0=ALU.mult, op1=ALU.add))
            powers(slice(1, 2), s0[:, 1:2], T_TOP)
            v.tensor_tensor(ft[:, :], sc[:, 1:2], si[:, 0:1], ALU.mult).then_inc(a_scale, 1)
            v.tensor_scalar(esc[:, :], si[:, 1:2], SCALE, None, ALU.mult)
            v.tensor_scalar(ta[:, :], ta[:, :], sc[:, 1:2], None, ALU.mult).then_inc(ta_ready, 1)
            for i in range(2, CT):
                stats(b0, i)
            dve.wait_ge(ah_done, 1)
            v.scalar_tensor_tensor(out=al[:, :, :], in0=at32, scalar=sc[:, 0:1], in1=ah[:, :, :],
                                   op0=ALU.mult, op1=ALU.subtract).then_inc(a_split, 1)
            for i in range(CT, 2 * CT):
                stats(b0, i)
            dve.wait_ge(stat_step, 1)
            norm_a(b0)
            norm_b(b0)
            norm_c(b0)
            dve.wait_ge(rs_ready, 1)
            for c in range(CT):
                if c >= 1:
                    dve.wait_ge(xl_done, c)
                v.tensor_scalar(xf[:, c % 2, :], xs[0][:, c, :], rs[:, c:c + 1], nb[:, c:c + 1],
                                ALU.mult, ALU.add).then_inc(xf_done, 1)
                x_low(b0, c)
            dve.wait_ge(bt_read, CT)
            v.tensor_reduce(bm[:, :], bt32, axis=AX.XY, op=ALU.max, apply_absolute_value=True).then_inc(bm_ready, 1)
            dve.wait_ge(wv_in, 16)
            bias_dots(2)
            dve.wait_ge(bsmax, 1)
            link(v.tensor_scalar(s0[:, 2:3], bmr[:, :], 1e-30, None, ALU.max))
            powers(slice(2, 3), s0[:, 2:3], W_TOP)
            v.tensor_scalar(cu[:, :], si[:, 2:3], 1.0 / U_SCALE, None, ALU.mult).then_inc(b_scale, 1)
            for i in range(CT):
                t_low(b0, i)
            dve.wait_ge(bh_done, 1)
            v.scalar_tensor_tensor(out=bl[:, :, :], in0=bt32, scalar=sc[:, 2:3], in1=bh[:, :, :],
                                   op0=ALU.mult, op1=ALU.subtract).then_inc(scratch_free, 1)
            t_low(b0, 4)
            tile_sums(vec_o, w_pt, 2, vo_ready)
            t_low(b0, 5)
            tile_sums(vec[:, 1, :], w_qkv[1], 0, vo_ready)
            t_low(b0, 6)
            link(v.tensor_tensor(prod[:, :], bt[:, 0:CT], bt[:, CT:2 * CT], ALU.mult))
            v.tensor_reduce(prod1[:, :], prod[:, :], axis=AX.X, op=ALU.add).then_inc(vo_ready, 1)
            t_low(b0, 7)
            for i in range(VO_AT):
                u_low(b0, i, bank[(PER["t"] + i) % MB])
            dve.wait_ge(projb_in, 16)
            dve.wait_ge(vo_full, 1)
            link(v.tensor_tensor(obias[:, :], ps_vb[:, 0:CT], projb[:, :], ALU.add))
            link(v.tensor_tensor(gw[:, :], ps_vb[:, CT:2 * CT], gam[:, :], ALU.mult))
            link(v.tensor_scalar(gw[:, :], gw[:, :], sc[:, 1:2], None, ALU.mult))
            link(v.tensor_scalar(gc[:, :], ps_vb[:, 2 * CT:2 * CT + 1], sc[:, 1:2], None, ALU.mult))
            for i in range(VO_AT, VO_AT + 2):
                u_low(b0, i, bank[(PER["t"] + i) % MB])
            g_columns(b0)
            for i in range(VO_AT + 2, PER["u"]):
                u_low(b0, i, bank[(PER["t"] + i) % MB])

            def one(b, last):
                bn = nxt(b)
                seq = LAST if last else BATCH
                bk = {g: bank[(BASE + n) % MB] for n, g in enumerate(seq)}
                if not last:
                    for i in range(2 * CT):
                        stats(bn, i)
                    wait(dve, stat_step, STATS, bn, 1)
                max_part(b, 0, 1)
                if not last:
                    norm_a(bn)
                    norm_b(bn)
                max_part(b, 0, 2)
                if not last:
                    norm_c(bn)
                max_part(b, 0, 3)
                max_pair(b, 0)
                max_all(b, 0)
                sub(b, 0, 0)
                sub(b, 0, 1)
                if not last:
                    x_low(bn, 0)
                    x_low(bn, 1)
                sub(b, 0, 2)
                sub(b, 0, 3)
                if not last:
                    x_low(bn, 2)
                    x_low(bn, 3)
                split(b, 0, 0)
                split(b, 0, 1)
                max_part(b, 1, 1)
                if last:
                    split(b, 0, 2)
                max_part(b, 1, 2)
                if last:
                    split(b, 0, 3)
                    inverse(b, 0)
                max_part(b, 1, 3)
                max_pair(b, 1)
                max_all(b, 1)
                for step in (() if last else
                             ("T0", "T1", "P2", "T2", "P3", "T3", "B0", "B1", "T4", "T5", "B2", "B3", "T6", "T7")):
                    n = int(step[1])
                    if step[0] == "T":
                        t_low(bn, n)
                    elif step[0] == "P":
                        split(b, 0, n)
                    else:
                        sub(b, 1, n)
                if last:
                    for k in range(NK):
                        sub(b, 1, k)
                if not last:
                    inverse(b, 0)
                split(b, 1, 0)
                split(b, 1, 1)
                if not last:
                    out_group(b, 0, bk["o", 0])
                split(b, 1, 2)
                if not last:
                    out_group(b, 1, bk["o", 1])
                split(b, 1, 3)
                if last:
                    out_group(b, 0, bk["o", 0])
                    out_group(b, 1, bk["o", 1])
                inverse(b, 1)
                for i in range(2, PER["o"]):
                    out_group(b, i, bk["o", i])
                if not last:
                    g_columns(bn)
                    for i in range(PER["u"]):
                        u_low(bn, i, bk["u", i])

            batches(dve, one)

        @block.tensor
        def _(pe):
            mm = nc.tensor.matmul

            def three(dst, parts, n):
                for k in range(n):
                    (wh, wl), (mh, ml) = parts(k)
                    mm(dst, wh, mh, start=(k == 0), stop=False)
                    mm(dst, wh, ml, start=False, stop=False)
                    ins = mm(dst, wl, mh, start=False, stop=(k == n - 1))
                return ins

            def t_group(bn, i, dst):
                ct, mh = i // NH, i % NH
                p = parity(bn)
                w, m = slice(ct * P, ct * P + P), slice(mh * H, mh * H + H)

                def parts(k):
                    if i == 0:
                        wait(pe, xl_done, CT, bn, k + 1)
                    return (ah[:, k, w], al[:, k, w]), (xh[p][:, k, m], xl[p][:, k, m])

                three(dst[:, :], parts, CT).then_inc(full["t"], 1)

            def u_group(bn, i, dst):
                p = parity(bn)
                w = slice(i * P, i * P + P)
                three(dst[:, :], lambda k: ((xh[p][:, k, w], xl[p][:, k, w]), (bh[:, k, :], bl[:, k, :])),
                      CT).then_inc(full["u"], 1)

            def s_group(b, i, dst):
                h, mt = i // MT, i % MT
                p = parity(b)
                if i == 0:
                    wait(pe, tl_done, PER["t"], b, PER["t"])
                w, n = slice(mt * P, mt * P + P), slice(h * H, h * H + H)
                three(dst[:, :], lambda k: ((th[:, k, w], tl[:, k, w]), (xh[p][:, k, n], xl[p][:, k, n])),
                      CT).then_inc(full["s"], 1)

            def o_group(b, i, dst):
                h, c = i // CT, i % CT
                w = slice(c * P, c * P + P)
                if i == 0:
                    wait(pe, evac["u"], PER["u"], b, PER["u"])
                for mt in range(MT):
                    hi, lo = chunk(h, mt // KC)
                    n = slice((mt % KC) * H, (mt % KC) * H + H)
                    if c == 0 and mt % KC == 0:
                        wait(pe, pl_done, NH * NK, b, NK * h + mt // KC + 1)
                    mm(dst[:, :], uh[:, mt, w], hi[:, n], start=(mt == 0), stop=False)
                    mm(dst[:, :], uh[:, mt, w], lo[:, n], start=False, stop=False)
                    ins = mm(dst[:, :], ul[:, mt, w], hi[:, n], start=False, stop=(mt == MT - 1))
                ins.then_inc(full["o"], 1)

            def group_means(bn):
                wait(pe, stat_step, STATS, bn, 2)
                mm(ps_small[:, 0:CT], gmean[:, :], mv[:, :, 0], start=True, stop=True).then_inc(stat_pe, 1)

            def group_vars(bn):
                wait(pe, stat_step, STATS, bn, 6)
                mm(ps_small[:, CT:2 * CT], gmean[:, :], dev[:, :], start=True, stop=True).then_inc(stat_pe, 1)

            b0 = (None, 0)
            pe.wait_ge(consts, 4)
            wq, wk, wv = w_qkv
            for o in range(CT):
                pe.wait_ge(wqk_in[o], 32)
                for t in range(CT):
                    ins = mm(bank[t][:, :], wk[:, o, t * P:t * P + P], wq[:, o, :], start=(o == 0), stop=(o == CT - 1))
                    if o == CT - 1:
                        ins.then_inc(set_full, 1)
            pe.wait_ge(vec_ready, 1)
            for t in range(CT):
                ins = mm(ps_va[:, t:t + 1], vec[:, 0, t * P:t * P + P], ones[:, 0:1], start=True, stop=True)
            ins.then_inc(vec_full, 1)
            pe.wait_ge(wp_in, 16)
            for t in range(CT):
                g = CT + t
                if g >= MB:
                    pe.wait_ge(at_read, g - MB + 1)
                for o in range(CT):
                    ins = nc.tensor.transpose(bank[g % MB][:, o * P:o * P + P], w_p[:, o, t * P:t * P + P], ident[:, :])
                ins.then_inc(set_full, 1)
            pe.wait_ge(wv_in, 16)
            pe.wait_ge(wpt_read, CT)
            pe.wait_ge(at_read, CT)
            for t in range(CT):
                for o in range(CT):
                    ins = mm(bank[(2 * CT + t) % MB][:, :], wv[:, o, t * P:t * P + P], w_pt[:, o, :],
                             start=(o == 0), stop=(o == CT - 1))
                    if (t, o) == (2, 1):
                        group_means(b0)
                    if (t, o) == (2, 3):
                        group_vars(b0)
                ins.then_inc(set_full, 1)

            pe.wait_ge(a_split, 1)
            pe.wait_ge(bt_read, CT)
            for k in range(CT):
                pe.wait_ge(xl_done, k + 1)
                for i in range(CT):
                    w, m = slice((i // NH) * P, (i // NH) * P + P), slice((i % NH) * H, (i % NH) * H + H)
                    mm(bank[i][:, :], ah[:, k, w], xh[0][:, k, m], start=(k == 0), stop=False)
                    mm(bank[i][:, :], ah[:, k, w], xl[0][:, k, m], start=False, stop=False)
                    ins = mm(bank[i][:, :], al[:, k, w], xh[0][:, k, m], start=False, stop=(k == CT - 1))
                    if k == CT - 1:
                        ins.then_inc(full["t"], 1)
            for g in range(CT, len(PROLOGUE)):
                kind, i = PROLOGUE[g]
                if g >= MB:
                    k, j = PROLOGUE[g - MB]
                    pe.wait_ge(evac[k], j + 1)
                if (kind, i) == ("u", 0):
                    pe.wait_ge(scratch_free, 1)
                if (kind, i) == ("u", VO_AT):
                    pe.wait_ge(vo_ready, 3)
                    for t in range(CT):
                        mm(ps_vb[:, t:t + 1], vec_o[:, t * P:t * P + P], ones[:, 0:1], start=True, stop=True)
                        mm(ps_vb[:, CT + t:CT + t + 1], vec[:, 1, t * P:t * P + P], ones[:, 0:1], start=True, stop=True)
                    mm(ps_vb[:, 2 * CT:2 * CT + 1], ones[:, :], prod1[:, :], start=True, stop=True).then_inc(vo_full, 1)
                (t_group if kind == "t" else u_group)(b0, i, bank[g % MB])

            def one(b, last):
                bn = nxt(b)
                seq = LAST if last else BATCH
                for n, (kind, i) in enumerate(seq):
                    if n >= MB:
                        k, j = seq[n - MB]
                        if k in "so":
                            wait(pe, evac[k], PER[k], b, j + 1)
                        else:
                            wait(pe, evac[k], PER[k], bn, j + 1)
                    else:
                        k, j = BATCH[n - MB]
                        wait(pe, evac[k], PER[k], b, j + 1)
                    dst = bank[(BASE + n) % MB]
                    if kind == "s":
                        s_group(b, i, dst)
                        if i == 4 and not last:
                            group_means(bn)
                        if i == 6 and not last:
                            group_vars(bn)
                    elif kind == "t":
                        t_group(bn, i, dst)
                    elif kind == "o":
                        o_group(b, i, dst)
                    else:
                        u_group(bn, i, dst)

            batches(pe, one)


_INS = ["x", "L0_conv_gamma", "L0_conv_beta", "L0_conv_qkv_w", "L0_conv_qkv_b", "L0_conv_proj_w", "L0_conv_proj_b"]


def kernel(**inputs):
    import numpy as _np
    import concourse.bacc as _bacc
    from concourse import mybir as _mybir
    from concourse.bass_utils import run_bass_kernel_spmd as _run

    nc = _bacc.Bacc("TRN2", target_bir_lowering=False, num_devices=1)
    arrays, args = {}, []
    for name in _INS:
        a = _np.ascontiguousarray(inputs[name])
        arrays[f"in_{name}"] = a
        args.append(nc.dram_tensor(f"in_{name}", a.shape, _mybir.dt.from_np(a.dtype), kind="ExternalInput").ap())
    shape = arrays["in_x"].shape
    args.append(nc.dram_tensor("out_0", shape, _mybir.dt.float32, kind="ExternalOutput").ap())
    attention_block_kernel(nc, *args)
    r = _run(nc, [arrays], core_ids=[0])
    return r.results[0]["out_0"]
```
